# Optimizing a Trainium2 kernel written in Bass

```python
import numpy as np
import jax
import jax.numpy as jnp

def _softmax(x, axis=-1):
    return jax.nn.softmax(x, axis=axis)

def _gelu(x):
    return jax.nn.gelu(x, approximate=True)

def _silu(x):
    return jax.nn.silu(x)

def _sigmoid(x):
    return jax.nn.sigmoid(x)

def _layernorm(x, axis=-1, eps=1e-05):
    m = jnp.mean(x, axis=axis, keepdims=True)
    v = jnp.var(x, axis=axis, keepdims=True)
    return (x - m) / jnp.sqrt(v + eps)

def _scatter_add(tgt, idx, src, axis=0):
    return tgt.at[idx].add(src)

def _segment_sum(src, seg, n):
    return jax.ops.segment_sum(src, seg, n)
kernel_name = 'mk_adaln_d1_jaxref_r8_ce9e51'

def setup_inputs(seed: int=0):
    np.random.seed(seed)
    _w = jnp.asarray

    def _L0_attn_setup():
        import jax, jax.numpy as jnp
        import numpy as np
        DT_MAX = 10.0
        RATE_EPS = 0.0001

        def _ssm_forward(x, W_in, W_state, W_dt, b_dt, A_log, W_C, D, W_out):
            B, L, d_model = x.shape
            ug = jnp.einsum('bld,ed->ble', x, W_in)
            u, gate = jnp.split(ug, 2, axis=-1)
            b_t = jnp.einsum('bld,nd->bln', u, W_state)
            dt_t = jnp.minimum(jax.nn.softplus(jnp.einsum('bld,nd->bln', u, W_dt) + b_dt), DT_MAX)
            rate = jax.nn.softplus(A_log) + RATE_EPS
            decay = jnp.clip(jnp.exp(-dt_t * rate), 0.0, 1.0)

            def step(h, inp):
                d_t, bt = inp
                h = d_t * h + (1.0 - d_t) * bt
                return (h, h)
            h0 = jnp.zeros((B, b_t.shape[-1]), x.dtype)
            xs = (jnp.swapaxes(decay, 0, 1), jnp.swapaxes(b_t, 0, 1))
            _, hs = jax.lax.scan(step, h0, xs)
            hs = jnp.swapaxes(hs, 0, 1)
            y = jnp.einsum('bln,dn->bld', hs, W_C)
            z = y * jax.nn.silu(gate) + x * D
            return jnp.einsum('bld,ed->ble', z, W_out)
        key = jax.random.key(seed)
        ks = jax.random.split(key, 8)
        B, L, D_MODEL, D_STATE = (4, 256, 128, 128)
        s = lambda fan_in: 1.0 / np.sqrt(fan_in)
        return {'x': jax.random.normal(ks[0], (B, L, D_MODEL), jnp.float32), 'W_in': jax.random.normal(ks[1], (2 * D_MODEL, D_MODEL), jnp.float32) * s(D_MODEL), 'W_state': jax.random.normal(ks[2], (D_STATE, D_MODEL), jnp.float32) * s(D_MODEL), 'W_dt': jax.random.normal(ks[3], (D_STATE, D_MODEL), jnp.float32) * s(D_MODEL), 'b_dt': jax.random.normal(ks[4], (D_STATE,), jnp.float32) * s(D_MODEL), 'A_log': jnp.zeros((D_STATE,), jnp.float32), 'W_C': jax.random.normal(ks[5], (D_MODEL, D_STATE), jnp.float32) * s(D_STATE), 'D': jnp.ones((D_MODEL,), jnp.float32), 'W_out': jax.random.normal(ks[6], (D_MODEL, D_MODEL), jnp.float32) * s(D_MODEL)}
    _L0_attn_in = _L0_attn_setup()

    def _L0_ffn_setup():
        import jax, jax.numpy as jnp
        import numpy as np
        from math import sqrt
        B, S, D, H, E, K, FF = (2, 128, 128, 16, 8, 2, 512)
        HD = D // H
        EPS = 1e-05

        def _rope_cache(seq_len, hd):
            inv_freq = 1.0 / 10000.0 ** (jnp.arange(0, hd, 2, dtype=jnp.float32) / hd)
            t = jnp.arange(seq_len, dtype=jnp.float32)
            freqs = t[:, None] * inv_freq[None, :]
            emb = jnp.concatenate([freqs, freqs], axis=-1)
            return (jnp.cos(emb), jnp.sin(emb))

        def _rotate_half(x):
            x1, x2 = jnp.split(x, 2, axis=-1)
            return jnp.concatenate([-x2, x1], axis=-1)

        def _layernorm(x, g, b):
            m = jnp.mean(x, axis=-1, keepdims=True)
            v = jnp.var(x, axis=-1, keepdims=True)
            return (x - m) * jax.lax.rsqrt(v + EPS) * g + b

        def _forward(x, Wq, bq, Wk, bk, Wv, bv, Wo, bo, Wg, bg, W1, b1, W2, b2, g1, be1, g2, be2):
            bsz, seq, d = x.shape
            q = (x @ Wq + bq).reshape(bsz, seq, H, HD).transpose(0, 2, 1, 3)
            k = (x @ Wk + bk).reshape(bsz, seq, H, HD).transpose(0, 2, 1, 3)
            v = (x @ Wv + bv).reshape(bsz, seq, H, HD).transpose(0, 2, 1, 3)
            cos, sin = _rope_cache(seq, HD)
            cos = cos[None, None]
            sin = sin[None, None]
            q = q * cos + _rotate_half(q) * sin
            k = k * cos + _rotate_half(k) * sin
            scores = jnp.einsum('bhqd,bhkd->bhqk', q, k) / sqrt(HD)
            attn = jax.nn.softmax(scores, axis=-1)
            ao = jnp.einsum('bhqk,bhkd->bhqd', attn, v)
            ao = ao.transpose(0, 2, 1, 3).reshape(bsz, seq, d)
            attn_out = ao @ Wo + bo
            x1 = _layernorm(x + attn_out, g1, be1)
            gate_logits = x1 @ Wg + bg
            gate_probs = jax.nn.softmax(gate_logits, axis=-1)
            topk_p, topk_i = jax.lax.top_k(gate_probs, K)
            topk_p = topk_p / jnp.sum(topk_p, axis=-1, keepdims=True)
            comb = jnp.sum(jax.nn.one_hot(topk_i, E, dtype=x.dtype) * topk_p[..., None], axis=-2)
            h = jax.nn.gelu(jnp.einsum('bsd,edf->bsef', x1, W1) + b1, approximate=False)
            y = jnp.einsum('bsef,efd->bsed', h, W2) + b2
            moe_out = jnp.einsum('bse,bsed->bsd', comb, y)
            return _layernorm(x1 + moe_out, g2, be2)
        key = jax.random.key(seed)
        ks = jax.random.split(key, 20)
        std = 0.02
        p = lambda k, sh: jax.random.normal(k, sh, dtype=jnp.float32) * std
        return {'x': jax.random.normal(ks[0], (B, S, D), dtype=jnp.float32), 'Wq': p(ks[1], (D, D)), 'bq': jnp.zeros((D,), jnp.float32), 'Wk': p(ks[2], (D, D)), 'bk': jnp.zeros((D,), jnp.float32), 'Wv': p(ks[3], (D, D)), 'bv': jnp.zeros((D,), jnp.float32), 'Wo': p(ks[4], (D, D)), 'bo': jnp.zeros((D,), jnp.float32), 'Wg': p(ks[5], (D, E)), 'bg': jnp.zeros((E,), jnp.float32), 'W1': p(ks[6], (E, D, FF)), 'b1': jnp.zeros((E, FF), jnp.float32), 'W2': p(ks[7], (E, FF, D)), 'b2': jnp.zeros((E, D), jnp.float32), 'g1': jnp.ones((D,), jnp.float32), 'be1': jnp.zeros((D,), jnp.float32), 'g2': jnp.ones((D,), jnp.float32), 'be2': jnp.zeros((D,), jnp.float32)}
    _L0_ffn_in = _L0_ffn_setup()
    _L0_c = _w((lambda *s: np.random.randn(*s).astype(np.float32) * 0.05)(8, 128))
    _L0_wmod = _w((lambda *s: np.random.randn(*s).astype(np.float32) * 0.05)(128, 6 * 128) * 128 ** (-0.5))
    _d = {'L0_attn_x': _L0_attn_in['x'], 'L0_attn_W_in': _L0_attn_in['W_in'], 'L0_attn_W_state': _L0_attn_in['W_state'], 'L0_attn_W_dt': _L0_attn_in['W_dt'], 'L0_attn_b_dt': _L0_attn_in['b_dt'], 'L0_attn_A_log': _L0_attn_in['A_log'], 'L0_attn_W_C': _L0_attn_in['W_C'], 'L0_attn_D': _L0_attn_in['D'], 'L0_attn_W_out': _L0_attn_in['W_out'], 'L0_ffn_Wq': _L0_ffn_in['Wq'], 'L0_ffn_bq': _L0_ffn_in['bq'], 'L0_ffn_Wk': _L0_ffn_in['Wk'], 'L0_ffn_bk': _L0_ffn_in['bk'], 'L0_ffn_Wv': _L0_ffn_in['Wv'], 'L0_ffn_bv': _L0_ffn_in['bv'], 'L0_ffn_Wo': _L0_ffn_in['Wo'], 'L0_ffn_bo': _L0_ffn_in['bo'], 'L0_ffn_Wg': _L0_ffn_in['Wg'], 'L0_ffn_bg': _L0_ffn_in['bg'], 'L0_ffn_W1': _L0_ffn_in['W1'], 'L0_ffn_b1': _L0_ffn_in['b1'], 'L0_ffn_W2': _L0_ffn_in['W2'], 'L0_ffn_b2': _L0_ffn_in['b2'], 'L0_ffn_g1': _L0_ffn_in['g1'], 'L0_ffn_be1': _L0_ffn_in['be1'], 'L0_ffn_g2': _L0_ffn_in['g2'], 'L0_ffn_be2': _L0_ffn_in['be2'], 'L0_c': _L0_c, 'L0_wmod': _L0_wmod}
    _x0 = _d['L0_attn_x']
    _d['L0_attn_x'] = jax.random.normal(jax.random.fold_in(jax.random.key(seed), 1), (8, 512, 128), dtype=_x0.dtype)
    del _x0
    return _d

def reference(L0_attn_x, L0_attn_W_in, L0_attn_W_state, L0_attn_W_dt, L0_attn_b_dt, L0_attn_A_log, L0_attn_W_C, L0_attn_D, L0_attn_W_out, L0_ffn_Wq, L0_ffn_bq, L0_ffn_Wk, L0_ffn_bk, L0_ffn_Wv, L0_ffn_bv, L0_ffn_Wo, L0_ffn_bo, L0_ffn_Wg, L0_ffn_bg, L0_ffn_W1, L0_ffn_b1, L0_ffn_W2, L0_ffn_b2, L0_ffn_g1, L0_ffn_be1, L0_ffn_g2, L0_ffn_be2, L0_c, L0_wmod):

    def _L0_attn_ref(x, W_in, W_state, W_dt, b_dt, A_log, W_C, D, W_out):
        import jax, jax.numpy as jnp
        import numpy as np
        DT_MAX = 10.0
        RATE_EPS = 0.0001

        def _ssm_forward(x, W_in, W_state, W_dt, b_dt, A_log, W_C, D, W_out):
            B, L, d_model = x.shape
            ug = jnp.einsum('bld,ed->ble', x, W_in)
            u, gate = jnp.split(ug, 2, axis=-1)
            b_t = jnp.einsum('bld,nd->bln', u, W_state)
            dt_t = jnp.minimum(jax.nn.softplus(jnp.einsum('bld,nd->bln', u, W_dt) + b_dt), DT_MAX)
            rate = jax.nn.softplus(A_log) + RATE_EPS
            decay = jnp.clip(jnp.exp(-dt_t * rate), 0.0, 1.0)

            def step(h, inp):
                d_t, bt = inp
                h = d_t * h + (1.0 - d_t) * bt
                return (h, h)
            h0 = jnp.zeros((B, b_t.shape[-1]), x.dtype)
            xs = (jnp.swapaxes(decay, 0, 1), jnp.swapaxes(b_t, 0, 1))
            _, hs = jax.lax.scan(step, h0, xs)
            hs = jnp.swapaxes(hs, 0, 1)
            y = jnp.einsum('bln,dn->bld', hs, W_C)
            z = y * jax.nn.silu(gate) + x * D
            return jnp.einsum('bld,ed->ble', z, W_out)
        return _ssm_forward(x, W_in, W_state, W_dt, b_dt, A_log, W_C, D, W_out)

    def _L0_ffn_ref(x, Wq, bq, Wk, bk, Wv, bv, Wo, bo, Wg, bg, W1, b1, W2, b2, g1, be1, g2, be2):
        import jax, jax.numpy as jnp
        import numpy as np
        from math import sqrt
        B, S, D, H, E, K, FF = (2, 128, 128, 16, 8, 2, 512)
        HD = D // H
        EPS = 1e-05

        def _rope_cache(seq_len, hd):
            inv_freq = 1.0 / 10000.0 ** (jnp.arange(0, hd, 2, dtype=jnp.float32) / hd)
            t = jnp.arange(seq_len, dtype=jnp.float32)
            freqs = t[:, None] * inv_freq[None, :]
            emb = jnp.concatenate([freqs, freqs], axis=-1)
            return (jnp.cos(emb), jnp.sin(emb))

        def _rotate_half(x):
            x1, x2 = jnp.split(x, 2, axis=-1)
            return jnp.concatenate([-x2, x1], axis=-1)

        def _layernorm(x, g, b):
            m = jnp.mean(x, axis=-1, keepdims=True)
            v = jnp.var(x, axis=-1, keepdims=True)
            return (x - m) * jax.lax.rsqrt(v + EPS) * g + b

        def _forward(x, Wq, bq, Wk, bk, Wv, bv, Wo, bo, Wg, bg, W1, b1, W2, b2, g1, be1, g2, be2):
            bsz, seq, d = x.shape
            q = (x @ Wq + bq).reshape(bsz, seq, H, HD).transpose(0, 2, 1, 3)
            k = (x @ Wk + bk).reshape(bsz, seq, H, HD).transpose(0, 2, 1, 3)
            v = (x @ Wv + bv).reshape(bsz, seq, H, HD).transpose(0, 2, 1, 3)
            cos, sin = _rope_cache(seq, HD)
            cos = cos[None, None]
            sin = sin[None, None]
            q = q * cos + _rotate_half(q) * sin
            k = k * cos + _rotate_half(k) * sin
            scores = jnp.einsum('bhqd,bhkd->bhqk', q, k) / sqrt(HD)
            attn = jax.nn.softmax(scores, axis=-1)
            ao = jnp.einsum('bhqk,bhkd->bhqd', attn, v)
            ao = ao.transpose(0, 2, 1, 3).reshape(bsz, seq, d)
            attn_out = ao @ Wo + bo
            x1 = _layernorm(x + attn_out, g1, be1)
            gate_logits = x1 @ Wg + bg
            gate_probs = jax.nn.softmax(gate_logits, axis=-1)
            topk_p, topk_i = jax.lax.top_k(gate_probs, K)
            topk_p = topk_p / jnp.sum(topk_p, axis=-1, keepdims=True)
            comb = jnp.sum(jax.nn.one_hot(topk_i, E, dtype=x.dtype) * topk_p[..., None], axis=-2)
            h = jax.nn.gelu(jnp.einsum('bsd,edf->bsef', x1, W1) + b1, approximate=False)
            y = jnp.einsum('bsef,efd->bsed', h, W2) + b2
            moe_out = jnp.einsum('bse,bsed->bsd', comb, y)
            return _layernorm(x1 + moe_out, g2, be2)
        return _forward(x, Wq, bq, Wk, bk, Wv, bv, Wo, bo, Wg, bg, W1, b1, W2, b2, g1, be1, g2, be2)
    x = L0_attn_x
    mod = (_silu(L0_c) @ L0_wmod).reshape(L0_c.shape[0], 6, 1, -1)
    sa, ca, ga, sb, cb, gb = (mod[:, 0], mod[:, 1], mod[:, 2], mod[:, 3], mod[:, 4], mod[:, 5])
    ga = (2 * (ga >= 0) - 1) * jnp.maximum(jnp.abs(ga), 0.25)
    gb = (2 * (gb >= 0) - 1) * jnp.maximum(jnp.abs(gb), 0.25)
    h = _layernorm(x, axis=-1) * (1 + ca) + sa
    x = x + ga * _L0_attn_ref(h, L0_attn_W_in, L0_attn_W_state, L0_attn_W_dt, L0_attn_b_dt, L0_attn_A_log, L0_attn_W_C, L0_attn_D, L0_attn_W_out)
    h = _layernorm(x, axis=-1) * (1 + cb) + sb
    x = x + gb * _L0_ffn_ref(h, L0_ffn_Wq, L0_ffn_bq, L0_ffn_Wk, L0_ffn_bk, L0_ffn_Wv, L0_ffn_bv, L0_ffn_Wo, L0_ffn_bo, L0_ffn_Wg, L0_ffn_bg, L0_ffn_W1, L0_ffn_b1, L0_ffn_W2, L0_ffn_b2, L0_ffn_g1, L0_ffn_be1, L0_ffn_g2, L0_ffn_be2)
    return x

_drawn_inputs = setup_inputs


def setup_inputs(seed=0):
    import zlib

    import numpy as np

    out = dict(_drawn_inputs(seed))
    spreads = {'L0_attn_A_log': (0.0, 0.8),
     'L0_attn_D': (1.0, 0.2),
     'L0_ffn_bq': (0.0, 0.8),
     'L0_ffn_bk': (0.0, 0.8),
     'L0_ffn_bv': (0.0, 0.8),
     'L0_ffn_bo': (0.0, 0.333),
     'L0_ffn_bg': (0.0, 0.768),
     'L0_ffn_b1': (0.0, 0.8),
     'L0_ffn_b2': (0.0, 0.496),
     'L0_ffn_g1': (1.0, 0.2),
     'L0_ffn_be1': (0.0, 0.304),
     'L0_ffn_g2': (1.0, 0.2),
     'L0_ffn_be2': (0.0, 0.324)}
    factors = {'L0_attn_b_dt': 8.0,
     'L0_ffn_Wq': 8.0,
     'L0_ffn_Wk': 8.0,
     'L0_ffn_Wv': 8.0,
     'L0_ffn_Wo': 8.0,
     'L0_ffn_Wg': 3.411,
     'L0_ffn_W1': 6.212,
     'L0_ffn_W2': 5.547}
    for name, (base, spread) in spreads.items():
        noise = np.random.default_rng([zlib.crc32(name.encode()), seed]).standard_normal(out[name].shape)
        drawn = base * np.exp(spread * noise) if base else spread * noise
        out[name] = jnp.asarray(drawn.astype(out[name].dtype))
    for name, factor in factors.items():
        out[name] = (out[name] * factor).astype(out[name].dtype)
    return out
```

```python
from contextlib import ExitStack

import concourse.bass as bass
from concourse import mybir

ALU = mybir.AluOpType
ACT = mybir.ActivationFunctionType
AX = mybir.AxisListType
F32 = mybir.dt.float32
F32R = mybir.dt.float32r

P = 128
LN_EPS = 1e-5
RATE_EPS = 1e-4
DT_MAX = 10.0
DT_CLAMP = 20.0
MIN_GATE = 0.25
BANK = 512


class Queue:

    def __init__(self, sem):
        self.sem, self.count, self.steps, self.met = sem, 0, [], {}

    def wait(self, *marks):
        for sem, value in marks:
            if self.met.get(sem.name, 0) < value:
                self.met[sem.name] = value
                self.steps.append(lambda e, s=sem, v=value: e.wait_ge(s, v))

    def do(self, instruction, after=(), signal=True):
        self.wait(*after)
        if not signal:
            self.steps.append(instruction)
            return None
        self.count += 1
        self.steps.append(lambda e: instruction(e).then_inc(self.sem, 1))
        return (self.sem, self.count)

    def dma(self, stream, out, in_, after=()):
        self.wait(*after)
        stream.count += 16
        self.steps.append(lambda e: e.dma_start(out, in_).then_inc(stream.sem, 16))
        return (stream.sem, stream.count)

    def play(self, engine):
        for step in self.steps:
            step(engine)


class Stream:

    def __init__(self, sem):
        self.sem, self.count = sem, 0


class Slot:

    def __init__(self, ap):
        self.ap, self.free = ap, ()


class Ring:
    def __init__(self, slots):
        self.slots, self.n = slots, 0

    def take(self):
        self.n += 1
        return self.slots[(self.n - 1) % len(self.slots)]


def adaln_block(nc, a, out):
    B, L, D = a["x"].shape
    TB = L // P
    NT = B * TB
    H = 16
    HD = D // H
    G4 = 4
    E, _, FF = a["W1"].shape
    NF = FF // P
    SCORE_SCALE = float(HD) ** -0.5
    assert D == P and L == BANK and H == G4 * G4 and 3 * HD < 32

    x_tiles = a["x"].rearrange("b (i p) d -> b p i d", p=P)
    out_tiles = out.rearrange("b (i p) d -> b p i d", p=P)

    with ExitStack() as scope:
        sem = lambda name: scope.enter_context(nc.semaphore(name))
        pe, act, dve, pool, sp = (Queue(sem(n)) for n in ("pe_done", "act_done", "dve_done", "pool_done", "sp_done"))
        s_weights, s_x, s_stack, s_max, s_out0, s_out1, s_moe = (
            Stream(sem(n)) for n in ("weights_in", "x_in", "stacks_in", "max_in", "out_stored_even", "out_stored_odd", "moe_weights_in"))

        def sbuf(name, shape, dtype=F32, where=scope):
            return where.enter_context(nc.sbuf_tensor(name, shape, dtype))

        psum = scope.enter_context(nc.psum_tensor("psum", [P, 8, BANK], F32))
        banks = [Slot(psum[:, n, :]) for n in range(8)]

        X = sbuf("X", [P, NT, D])
        X1 = sbuf("X1", [P, NT, D])
        ident = sbuf("ident", [P, P])
        rows = sbuf("rows", [P, B, 4, D])
        GA, SB, CB, GB = 0, 1, 2, 3
        vec_names = ["b_dt", "A_log", "Dskip", "bq", "bq_rot", "bk", "bk_rot"]
        vecs = sbuf("vecs", [P, len(vec_names)])
        row_names = ["bo", "g1", "be1", "g2", "be2"]
        rowc = sbuf("rowc", [P, len(row_names), D])
        bg_row = sbuf("bg_row", [P, E])
        pri_row = sbuf("pri_row", [P, E])
        b1c = sbuf("b1c", [P, E, NF])
        b2m = sbuf("b2m", [E, D])
        Wg = sbuf("Wg", [P, E])
        Wqkv = sbuf("Wqkv", [P, 6, D])
        W_Q, W_QR, W_K, W_KR, W_V, W_O = range(6)
        W_INU, W_GATE, W_STATE, W_DT, W_C, W_OUT = range(6)
        cT = sbuf("cT", [P, B])
        modc = sbuf("modc", [P, 2, B])
        cos_t = sbuf("cos_t", [P, L])
        sin_t = sbuf("sin_t", [P, L])
        negrate = sbuf("negrate", [P, 1])
        half = sbuf("half", [P, TB])
        attn_row = sbuf("attn_row", [P, D])

        s0 = ExitStack()
        Wssm = sbuf("Wssm", [P, 6, D], where=s0)
        wmod = sbuf("wmod", [P, 6, D], where=s0)

        col = lambda name: vecs[:, vec_names.index(name):vec_names.index(name) + 1]
        row = lambda name: rowc[:, row_names.index(name), :]
        over_tiles = lambda ap: ap.unsqueeze(1).to_broadcast([P, TB, D])

        w = s_weights
        sp.dma(w, cT[:, :], a["cT"])
        sp.dma(w, wmod[:, :, :], a["wmod"].rearrange("c (n d) -> c n d", n=6))
        sp.dma(w, ident[:, :], a["ident"])
        for n, name in enumerate(vec_names):
            sp.dma(w, vecs[:, n:n + 1], a[name].rearrange("(p o) -> p o", o=1))
        for n, name in enumerate(("W_in_u", "W_gateT", "W_stateT", "W_dtT", "W_CT", "W_outT")):
            sp.dma(w, Wssm[:, n, :], a[name])
        for n, name in enumerate(("Wq", "Wq_rot", "Wk", "Wk_rot", "Wv", "Wo")):
            act.dma(w, Wqkv[:, n, :], a[name])
        for n, name in enumerate(row_names):
            act.dma(w, rowc[:, n, :], a[name].partition_broadcast(P))
        act.dma(w, bg_row[:, :], a["bg"].partition_broadcast(P))
        act.dma(w, pri_row[:, :], a["priority"].partition_broadcast(P))
        act.dma(w, b1c[:, :, :], a["b1T"])
        act.dma(w, b2m[:, :], a["b2"])
        act.dma(w, Wg[:, :], a["Wg"])
        act.dma(w, cos_t[:, :], a["cos"])
        weights_in = act.dma(w, sin_t[:, :], a["sin"])
        x_in = [sp.dma(s_x, X[:, b * TB:(b + 1) * TB, :], x_tiles[b]) for b in range(B)]
        x_all_in = x_in[-1]

        def chain(queue):
            last = [()]

            def step(instruction, after=()):
                mark = queue.do(instruction, [*last[0], *after])
                last[0] = (mark,)
                return mark
            return step

        def normalise(src, dst, stats, mv, rstd, after, free):
            marks = []
            for i in range(TB):
                seen = dve.do(lambda e, i=i: e.bn_stats(stats[:, i, :], src[:, i, :]), [*after, *free])
                marks.append(dve.do(lambda e, i=i: e.bn_aggr(mv[:, i, :], stats[:, i, :]), [seen]))
            with_eps = pool.do(lambda e: e.tensor_scalar(rstd[:, :], mv[:, :, 1], LN_EPS, None, ALU.add), [marks[-1]])
            powered = pool.do(lambda e: e.tensor_tensor(rstd[:, :], rstd[:, :], half[:, :], ALU.pow), [with_eps])
            for i in range(TB):
                done = dve.do(lambda e, i=i: e.tensor_scalar(
                    dst[:, i, :], src[:, i, :], mv[:, i, 0:1], rstd[:, i:i + 1], ALU.subtract, ALU.mult), [powered, *free])
            return done

        def transpose_tiles(src, bank, after):
            for i in range(TB):
                done = pe.do(lambda e, i=i: e.transpose(bank.ap[:, i * P:(i + 1) * P], src[:, i, :], ident[:, :]),
                             [*after, *bank.free], signal=i == TB - 1)
            return done

        half_set = dve.do(lambda e: e.memset(half[:, :], -0.5))
        if True:
            silu_c = sbuf("silu_c", [P, B], where=s0)
            silu_cb = sbuf("silu_cb", [P, B, P], where=s0)
            bv_b = sbuf("bv_b", [P, P], where=s0)
            bvc = sbuf("bvc", [P, 1], where=s0)
            ones = sbuf("ones", [P, P], where=s0)
            gsign = sbuf("gsign", [P, B, D], where=s0)
            gabs = sbuf("gabs", [P, B, D], where=s0)
            Wfused = sbuf("Wfused", [P, 2, D], where=s0)
            Wout_b = sbuf("Wout_b", [P, B, D], where=s0)
            rate3 = sbuf("rate3", [P, 3], where=s0)
            bv_in = sp.dma(s_moe, bvc[:, :], a["bv"].rearrange("(p o) -> p o", o=1))
            ones_set = dve.do(lambda e: e.memset(ones[:, :], 1.0))
            silued = act.do(lambda e: e.activation(silu_c[:, :], cT[:, :], ACT.Silu), [weights_in])
            for b in range(B):
                spread = dve.do(lambda e, b=b: e.tensor_scalar(silu_cb[:, b, :], ones[:, :], silu_c[:, b:b + 1], None, ALU.mult), [silued, ones_set])
            bv_spread = dve.do(lambda e: e.tensor_scalar(bv_b[:, :], ones[:, :], bvc[:, 0:1], None, ALU.mult), [bv_in])
            for n in range(2):
                mods = pe.do(lambda e, n=n: e.matmul(banks[0].ap[:, n * B:(n + 1) * B], wmod[:, n, :], silu_c[:, :], start=True, stop=True), [silued])
            mod_sa = dve.do(lambda e: e.tensor_copy(modc[:, 0, :], banks[0].ap[:, 0:B]), [mods])
            mod_ca = dve.do(lambda e: e.tensor_scalar(modc[:, 1, :], banks[0].ap[:, B:2 * B], 1.0, None, ALU.add), [mods])
            for b in range(B):
                bank = banks[b % 4 + 1]
                made = pe.do(lambda e, b=b, k=bank: e.matmul(k.ap, silu_cb[:, b, :], wmod[:, 2:6, :].rearrange("c n d -> c (n d)"),
                                                            start=True, stop=True), [spread, *bank.free])
                rows_in = dve.do(lambda e, b=b, k=bank: e.tensor_copy(rows[:, b, :, :].rearrange("p n d -> p (n d)"), k.ap), [made])
                bank.free = (rows_in,)
            rows_done = []
            for which in (GA, GB):
                g = rows[:, :, which, :]
                signed = dve.do(lambda e, g=g: e.tensor_scalar(gsign[:, :, :], g, 0.0, 2.0, ALU.is_ge, ALU.mult), [rows_in, *rows_done])
                sized = dve.do(lambda e, g=g: e.scalar_tensor_tensor(out=gabs[:, :, :], in0=g, scalar=-1.0, in1=g, op0=ALU.mult, op1=ALU.max), [rows_in, *rows_done])
                sized = dve.do(lambda e: e.tensor_scalar(gabs[:, :, :], gabs[:, :, :], MIN_GATE, None, ALU.max), [sized])
                rows_done = [dve.do(lambda e, g=g: e.scalar_tensor_tensor(
                    out=g, in0=gsign[:, :, :], scalar=-1.0, in1=gabs[:, :, :], op0=ALU.add, op1=ALU.mult), [signed, sized])]
            cb_done = dve.do(lambda e: e.tensor_scalar(rows[:, :, CB, :], rows[:, :, CB, :], 1.0, None, ALU.add), [rows_in])
            rows_ready = [*rows_done, cb_done]
            bv_wo = pe.do(lambda e: e.matmul(banks[5].ap[:, 0:D], bv_b[:, :], Wqkv[:, W_O, :], start=True, stop=True), [bv_spread])
            attn_row_done = dve.do(lambda e: e.tensor_tensor(attn_row[:, :], banks[5].ap[:, 0:D], row("bo"), ALU.add), [bv_wo])
            banks[5].free = (attn_row_done,)
            for n, wi in enumerate((W_STATE, W_DT)):
                fused = pe.do(lambda e, n=n, wi=wi: e.matmul(banks[6].ap[:, n * D:(n + 1) * D], Wssm[:, W_INU, :], Wssm[:, wi, :], start=True, stop=True), [weights_in])
            fused_in = dve.do(lambda e: e.tensor_copy(Wfused[:, :, :].rearrange("p n d -> p (n d)"), banks[6].ap[:, 0:2 * D]), [fused])
            banks[6].free = (fused_in,)
            banks[0].free = (mod_ca,)
            for b in range(B):
                wout_ready = dve.do(lambda e, b=b: e.tensor_tensor(Wout_b[:, b, :], Wssm[:, W_OUT, :], rows[:, b, GA, :], ALU.mult), rows_ready)
            v = chain(dve)
            v(lambda e: e.scalar_tensor_tensor(out=rate3[:, 0:1], in0=col("A_log"), scalar=-1.0, in1=col("A_log"), op0=ALU.mult, op1=ALU.min), [weights_in])
            r1 = v(lambda e: e.tensor_scalar(rate3[:, 1:2], col("A_log"), 0.0, None, ALU.max))

        with ExitStack() as sa:
            hT = sbuf("hT", [P, B, L], where=sa)
            gate = sbuf("gate", [P, B, L], where=sa)
            stats = sbuf("stats_a", [P, 2, TB, 6], where=sa)
            mv = sbuf("mv_a", [P, 2, TB, 2], where=sa)
            rstd = sbuf("rstd_a", [P, 2, TB], where=sa)
            xn = sbuf("xn_a", [P, 2, TB, D], where=sa)
            xn_free = [(), ()]
            gated = []
            hT_in = []
            for b in range(B):
                s = b % 2
                tiles = X[:, b * TB:(b + 1) * TB, :]
                normed = normalise(tiles, xn[:, s], stats[:, s], mv[:, s], rstd[:, s], [x_all_in, half_set], xn_free[s])
                bank = banks[s]
                turned = transpose_tiles(xn[:, s], bank, [normed])
                xn_free[s] = (turned,)
                modulated = dve.do(lambda e, b=b, k=bank: e.tensor_scalar(
                    hT[:, b, :], k.ap, modc[:, 1, b:b + 1], modc[:, 0, b:b + 1], ALU.mult, ALU.add), [turned, mod_sa, mod_ca])
                bank.free = (modulated,)
                hT_in.append(modulated)
                bank = banks[2 + s]
                product = pe.do(lambda e, b=b, k=bank: e.matmul(k.ap, Wssm[:, W_GATE, :], hT[:, b, :], start=True, stop=True), [modulated, *bank.free])
                gated.append(act.do(lambda e, b=b, k=bank: e.activation(gate[:, b, :], k.ap, ACT.Silu), [product]))
                bank.free = (gated[-1],)

            act.steps.append(lambda e: e.preload_act_table_set("natural_log_exp_and_others"))
            r2 = act.do(lambda e: e.activation(rate3[:, 2:3], rate3[:, 0:1], ACT.Exp), [r1])
            r3 = act.do(lambda e: e.activation(rate3[:, 2:3], rate3[:, 2:3], ACT.Ln, bias=1.0), [r2])
            r4 = dve.do(lambda e: e.tensor_tensor(rate3[:, 2:3], rate3[:, 2:3], rate3[:, 1:2], ALU.add), [r3])
            rate_ready = dve.do(lambda e: e.tensor_scalar(negrate[:, :], rate3[:, 2:3], RATE_EPS, -1.0, ALU.add, ALU.mult), [r4])

            work = {n: [sbuf(f"{n}_{i}", [P, L], where=sa) for i in range(2)] for n in ("dt", "ed", "drive", "state", "z")}
            work_free = {n: [(), ()] for n in work}
            x2_in = []
            for b in range(B):
                s = b % 2
                dt, ed, drive, state, z = (work[n][s] for n in ("dt", "ed", "drive", "state", "z"))
                bank_b, bank_dt = banks[s], banks[2 + s]
                p_dt = pe.do(lambda e, b=b, k=bank_dt: e.matmul(k.ap, Wfused[:, 1, :], hT[:, b, :], start=True, stop=True), [hT_in[b], fused_in, *bank_dt.free])
                p_b = pe.do(lambda e, b=b, k=bank_b: e.matmul(k.ap, Wfused[:, 0, :], hT[:, b, :], start=True, stop=True), [*bank_b.free])
                m = dve.do(lambda e, o=dt, k=bank_dt: e.tensor_scalar(o[:, :], k.ap, col("b_dt"), DT_CLAMP, ALU.add, ALU.min), [p_dt, *work_free["dt"][s]])
                bank_dt.free = (m,)
                m = act.do(lambda e, o=ed, i=dt: e.activation(o[:, :], i[:, :], ACT.Exp), [m, *work_free["ed"][s]])
                m = act.do(lambda e, o=dt, i=ed: e.activation(o[:, :], i[:, :], ACT.Ln, bias=1.0), [m])
                m = dve.do(lambda e, o=ed, i=dt: e.tensor_scalar(o[:, :], i[:, :], DT_MAX, negrate[:, 0:1], ALU.min, ALU.mult), [m, rate_ready])
                work_free["dt"][s] = (m,)
                m = act.do(lambda e, o=ed: e.activation(o[:, :], o[:, :], ACT.Exp), [m])
                m = dve.do(lambda e, o=ed: e.tensor_scalar(o[:, :], o[:, :], 0.0, 1.0, ALU.max, ALU.min), [m])
                m = dve.do(lambda e, o=drive, i=ed, k=bank_b: e.scalar_tensor_tensor(
                    out=o[:, :], in0=i[:, :], scalar=-1.0, in1=k.ap, op0=ALU.add, op1=ALU.mult), [m, p_b])
                bank_b.free = (m,)
                m = dve.do(lambda e, o=state, i=ed, j=drive: e.tensor_tensor_scan(
                    o[:, :], i[:, :], j[:, :], 0.0, ALU.mult, ALU.subtract), [m, *work_free["state"][s]])
                work_free["ed"][s] = (m,)
                bank_y = banks[4 + s]
                p_y = pe.do(lambda e, i=state, k=bank_y: e.matmul(k.ap, Wssm[:, W_C, :], i[:, :], start=True, stop=True), [m, *bank_y.free])
                work_free["state"][s] = (p_y,)
                m = dve.do(lambda e, b=b, o=z, k=bank_y: e.tensor_tensor(o[:, :], k.ap, gate[:, b, :], ALU.mult), [p_y, gated[b], *work_free["z"][s]])
                bank_y.free = (m,)
                m = dve.do(lambda e, b=b, o=z: e.scalar_tensor_tensor(
                    out=o[:, :], in0=hT[:, b, :], scalar=col("Dskip"), in1=o[:, :], op0=ALU.mult, op1=ALU.add), [m])
                bank_o = banks[6 + s]
                for i in range(TB):
                    p_o = pe.do(lambda e, b=b, i=i, z=z, k=bank_o: e.matmul(
                        k.ap[:, i * P:(i + 1) * P], z[:, i * P:(i + 1) * P], Wout_b[:, b, :], start=True, stop=True),
                        [m, wout_ready, *bank_o.free], signal=i == TB - 1)
                work_free["z"][s] = (p_o,)
                tiles = X[:, b * TB:(b + 1) * TB, :].rearrange("p i d -> p (i d)")
                m = dve.do(lambda e, t=tiles, k=bank_o: e.tensor_tensor(t, t, k.ap, ALU.add), [p_o])
                bank_o.free = (m,)
                x2_in.append(m)
            ssm_done = [x2_in[-1], p_o]
        s0.close()

        with ExitStack() as sb:
            HI1, HI2, LO, MAXROW = 0, HD, 2 * HD, 3 * HD
            QS = [sbuf(f"QS{i}", [P, G4, L], F32R, where=sb) for i in range(2)]
            KS = [sbuf(f"KS{i}", [P, H, L], F32R, where=sb) for i in range(2)]
            onesrow = sbuf("onesrow", [G4 * TB, P], where=sb)
            zrow = sbuf("zrow", [G4 * TB, P], where=sb)
            vaug = [sbuf(f"vaug{i}", [P, TB, H, 32], where=sb) for i in range(2)]
            PT = Ring([Slot(sbuf(f"PT{i}", [P, L], where=sb)) for i in range(8)])
            h2 = sbuf("h2", [P, 2, TB, D], where=sb)
            xn2 = sbuf("xn2", [P, TB, D], where=sb)
            h2T = sbuf("h2T", [P, L], where=sb)
            rope = [sbuf(f"rope{i}", [P, L], where=sb) for i in range(2)]
            hi = sbuf("hi", [P, 2, L], F32R, where=sb)
            lo = sbuf("lo", [P, 2, L], F32R, where=sb)
            negmax = sbuf("negmax", [P, 2, G4 * TB], where=sb)
            maxT = sbuf("maxT", [G4 * TB, 2, P], F32R, where=sb)
            oT = sbuf("oT", [P, 2, L], where=sb)
            rsum = sbuf("rsum", [P, TB, G4], where=sb)
            ao = sbuf("ao", [P, TB, D], where=sb)
            aoT = sbuf("aoT", [P, L], where=sb)
            stats = sbuf("stats_b", [P, 2, TB, 6], where=sb)
            mv = sbuf("mv_b", [P, 2, TB, 2], where=sb)
            rstd = sbuf("rstd_b", [P, 2, TB], where=sb)

            cleared = []
            for i in range(2):
                for t in (QS[i], KS[i]):
                    cleared.append(dve.do(lambda e, t=t: e.memset(t[:, :, :].bitcast(F32), 0.0), ssm_done))
                cleared.append(pool.do(lambda e, i=i: e.memset(vaug[i][:, :, :, :], 0.0), ssm_done))
                cleared.append(pool.do(lambda e, i=i: e.memset(vaug[i][:, :, :, HD:HD + 1], 1.0), [cleared[-1]]))
            cleared.append(dve.do(lambda e: e.memset(onesrow[:, :], 1.0), ssm_done))
            cleared.append(dve.do(lambda e: e.memset(zrow[:, :], 0.0), ssm_done))
            for i in range(2):
                for g in range(G4):
                    r = 32 * g + MAXROW
                    ones_in = sp.dma(s_stack, KS[i][r:r + 1, g * G4:(g + 1) * G4, :].bitcast(F32), onesrow[:, :], cleared)

            misc = Ring(banks[6:8])
            smax_banks, score_banks, pv_banks = Ring(banks[0:2]), Ring(banks[2:5]), Ring(banks[5:6])
            stack_read = [(), ()]
            v_read = [(), ()]
            h2_free = [(), ()]
            shared = {k: () for k in ("xn2", "h2T", "aoT", "ao", "rs", "hi0", "hi1", "max0", "max1", "oT0", "oT1")}
            rope_free = [(), ()]
            ready = {}

            def prepare(b):
                s = b % 2
                tiles = X[:, b * TB:(b + 1) * TB, :]
                normed = normalise(tiles, xn2, stats[:, 0], mv[:, 0], rstd[:, 0], [x2_in[b], *ssm_done], shared["xn2"])
                scaled = pool.do(lambda e: e.tensor_tensor(h2[:, s], xn2[:, :, :], over_tiles(rows[:, b, CB, :]), ALU.mult), [normed, *rows_ready, *h2_free[s]])
                h2_in = pool.do(lambda e: e.tensor_tensor(h2[:, s], h2[:, s], over_tiles(rows[:, b, SB, :]), ALU.add), [scaled])
                shared["xn2"] = (scaled,)
                yield
                bank = misc.take()
                turned = transpose_tiles(h2[:, s], bank, [h2_in])
                h2T_in = act.do(lambda e, k=bank: e.activation(h2T[:, :], k.ap, ACT.Copy), [turned, *shared["h2T"]])
                bank.free = (h2T_in,)
                yield
                bank = misc.take()
                for i in range(TB):
                    p_v = pe.do(lambda e, i=i, k=bank: e.matmul(k.ap[:, i * P:(i + 1) * P], h2T[:, i * P:(i + 1) * P], Wqkv[:, W_V, :], start=True, stop=True),
                                [h2T_in, *bank.free], signal=i == TB - 1)
                v_in = dve.do(lambda e, k=bank: e.tensor_copy(vaug[s][:, :, :, 0:HD], k.ap.rearrange("p (i h d) -> p i h d", i=TB, h=H)), [p_v, *cleared, *v_read[s]])
                bank.free = (v_in,)
                yield
                for n, (wp, wr, bp, br) in enumerate(((W_Q, W_QR, "bq", "bq_rot"), (W_K, W_KR, "bk", "bk_rot"))):
                    plain, turned_ = misc.take(), misc.take()
                    p_p = pe.do(lambda e, k=plain, wp=wp: e.matmul(k.ap, Wqkv[:, wp, :], h2T[:, :], start=True, stop=True), [h2T_in, *plain.free])
                    p_r = pe.do(lambda e, k=turned_, wr=wr: e.matmul(k.ap, Wqkv[:, wr, :], h2T[:, :], start=True, stop=True), [*turned_.free])
                    m1 = dve.do(lambda e, k=plain, bp=bp: e.scalar_tensor_tensor(
                        out=rope[0][:, :], in0=k.ap, scalar=col(bp), in1=cos_t[:, :], op0=ALU.add, op1=ALU.mult), [p_p, *rope_free[0]])
                    plain.free = (m1,)
                    m2 = dve.do(lambda e, k=turned_, br=br: e.scalar_tensor_tensor(
                        out=rope[1][:, :], in0=k.ap, scalar=col(br), in1=sin_t[:, :], op0=ALU.add, op1=ALU.mult), [p_r, *rope_free[1]])
                    turned_.free = (m2,)
                    m3 = pool.do(lambda e: e.tensor_tensor(rope[0][:, :], rope[0][:, :], rope[1][:, :], ALU.add), [m1, m2])
                    rope_free[1] = (m3,)
                    m4 = dve.do(lambda e, n=n: e.tensor_copy(hi[:, n, :], rope[0][:, :]), [m3, *shared[f"hi{n}"]])
                    m5 = pool.do(lambda e, n=n: e.tensor_tensor(lo[:, n, :], rope[0][:, :], hi[:, n, :].bitcast(F32), ALU.subtract), [m4, *shared[f"hi{n}"]])
                    rope_free[0] = (m5,)
                    rows_of = ((HI1, hi), (HI2, hi), (LO, lo)) if n == 0 else ((HI1, hi), (HI2, lo), (LO, hi))
                    for g in range(G4):
                        p = slice(32 * g, 32 * g + 32)
                        for r, part in rows_of:
                            r0 = 32 * g + r
                            dst = QS[s][r0:r0 + HD, :, :] if n == 0 else KS[s][r0:r0 + HD, g * G4:(g + 1) * G4, :]
                            stacked = sp.dma(s_stack, dst.bitcast(F32), part[p, n, :].bitcast(F32), [m4, m5, *cleared, *stack_read[s]])
                    if n == 0:
                        for g in range(G4):
                            r = 32 * g + MAXROW
                            stacked = sp.dma(s_stack, QS[s][r:r + 1, :, :].bitcast(F32), zrow[:, :])
                    shared[f"hi{n}"] = (stacked,)
                    if n == 1:
                        shared["h2T"] = (p_r,)
                    yield
                ready[b] = (stacked, v_in, h2_in)

            def find_max(b, g):
                s, t = b % 2, g % 2
                for G in range(G4):
                    h = g * G4 + G
                    for i in range(TB):
                        bank = smax_banks.take()
                        p_s = pe.do(lambda e, G=G, h=h, i=i, k=bank: e.matmul(k.ap, QS[s][:, G, i * P:(i + 1) * P], KS[s][:, h, :], start=True, stop=True),
                                    [ready[b][0], *bank.free])
                        n = G * TB + i
                        found = dve.do(lambda e, n=n, k=bank: e.tensor_reduce(negmax[:, t, n:n + 1], k.ap, AX.X, ALU.max, negate=True), [p_s, *shared[f"max{t}"]])
                        bank.free = (found,)
                        yield
                bank = misc.take()
                turned = pe.do(lambda e, k=bank: e.transpose(k.ap[0:G4 * TB, 0:P], negmax[:, t, :], ident[:, :]), [found, *bank.free])
                m = dve.do(lambda e, k=bank: e.tensor_copy(maxT[:, t, :], k.ap[0:G4 * TB, 0:P]), [turned, *shared[f"max{t}"]])
                bank.free = (m,)
                r = 32 * g + MAXROW
                sent = sp.dma(s_max, QS[s][r:r + 1, :, :].bitcast(F32), maxT[:, t, :].bitcast(F32), [m, turned])
                shared[f"max{t}"] = (sent,)
                return sent

            def attend(b, g, max_sent, side):
                s = b % 2
                acc = pv_banks.take()
                waiting = []

                def values(kt, slots):
                    nonlocal last
                    for G, (slot, mark) in enumerate(slots):
                        h = g * G4 + G
                        last = pe.do(lambda e, G=G, h=h, kt=kt, t=slot: e.matmul(
                            acc.ap[32 * G:32 * G + 32, :], vaug[s][:, kt, h, :], t.ap[:, :], start=kt == 0, stop=kt == TB - 1),
                            [mark, ready[b][1], *acc.free])
                        slot.free = (last,)
                last = None
                for kt in range(TB):
                    slots = []
                    for G in range(G4):
                        h = g * G4 + G
                        bank, slot = score_banks.take(), PT.take()
                        p_s = pe.do(lambda e, G=G, h=h, kt=kt, k=bank: e.matmul(k.ap, KS[s][:, h, kt * P:(kt + 1) * P], QS[s][:, G, :], start=True, stop=True),
                                    [max_sent, *bank.free])
                        m = act.do(lambda e, k=bank, t=slot: e.activation(t.ap[:, :], k.ap, ACT.Exp, scale=SCORE_SCALE), [p_s, *slot.free])
                        bank.free = (m,)
                        slots.append((slot, m))
                        next(side, None)
                    waiting.append((kt, slots))
                    if kt:
                        values(*waiting.pop(0))
                values(*waiting.pop(0))
                if g == G4 - 1:
                    v_read[s] = (last,)
                    stack_read[s] = (last,)
                return acc, last

            def collect(b, g, acc, last):
                t = g % 2
                m = act.do(lambda e, k=acc: e.activation(oT[:, t, :], k.ap, ACT.Copy), [last, *shared[f"oT{t}"]])
                acc.free = (m,)
                bank = misc.take()
                turned = transpose_tiles(oT[:, t, :].rearrange("p (i q) -> p i q", i=TB), bank, [m])
                shared[f"oT{t}"] = (turned,)
                o = bank.ap.rearrange("p (i j r) -> p i j r", i=TB, j=G4)
                m = dve.do(lambda e: e.reciprocal(rsum[:, :, :].unsqueeze(3), o[:, :, :, HD:HD + 1]), [turned, *shared["ao"], *shared["rs"]])
                dst = ao[:, :, 32 * g:32 * g + 32].rearrange("p i (j d) -> p i j d", j=G4)
                m = dve.do(lambda e: e.tensor_tensor(dst, o[:, :, :, 0:HD], rsum[:, :, :].unsqueeze(3).to_broadcast([P, TB, G4, HD]), ALU.mult), [m])
                bank.free = (m,)
                shared["rs"] = (m,)
                return m

            x1_in = {}

            def finish(b, done):
                s = b % 2
                bank = misc.take()
                turned = transpose_tiles(ao, bank, [done])
                shared["ao"] = (turned,)
                m = act.do(lambda e, k=bank: e.activation(aoT[:, :], k.ap, ACT.Copy), [turned, *shared["aoT"]])
                bank.free = (m,)
                yield
                bank = misc.take()
                for i in range(TB):
                    p_o = pe.do(lambda e, i=i, k=bank: e.matmul(k.ap[:, i * P:(i + 1) * P], aoT[:, i * P:(i + 1) * P], Wqkv[:, W_O, :], start=True, stop=True),
                                [m, *bank.free], signal=i == TB - 1)
                shared["aoT"] = (p_o,)
                h2s = h2[:, s].rearrange("p i d -> p (i d)")
                m = pool.do(lambda e: e.tensor_tensor(h2[:, s], h2[:, s], over_tiles(attn_row[:, :]), ALU.add), [ready[b][2], attn_row_done])
                m = dve.do(lambda e, k=bank: e.tensor_tensor(h2s, h2s, k.ap, ALU.add), [p_o, m])
                bank.free = (m,)
                yield
                dst = X1[:, b * TB:(b + 1) * TB, :]
                normed = normalise(h2[:, s], dst, stats[:, 1], mv[:, 1], rstd[:, 1], [m], ())
                h2_free[s] = (normed,)
                m = pool.do(lambda e: e.tensor_tensor(dst, dst, over_tiles(row("g1")), ALU.mult), [normed])
                x1_in[b] = pool.do(lambda e: e.tensor_tensor(dst, dst, over_tiles(row("be1")), ALU.add), [m])
                yield

            units = [(b, g) for b in range(B) for g in range(G4)]
            for _ in prepare(0):
                pass

            def drained(gen, box):
                box.append((yield from gen))

            box = {}
            box[0] = []
            for _ in drained(find_max(*units[0]), box[0]):
                pass
            extra = iter(())
            finishing = iter(())
            import itertools
            for n, (b, g) in enumerate(units):
                if g == 0:
                    extra = itertools.chain(finishing, prepare(b + 1) if b + 1 < B else iter(()))
                parts = []
                if g == G4 - 1:
                    for _ in extra:
                        pass
                else:
                    for _ in range(3):
                        next(extra, None)
                nxt = iter(())
                if n + 1 < len(units):
                    box[n + 1] = []
                    nxt = drained(find_max(*units[n + 1]), box[n + 1])
                acc, last = attend(b, g, box[n][0], nxt)
                for _ in nxt:
                    pass
                done = collect(b, g, acc, last)
                if g == G4 - 1:
                    finishing = finish(b, done)
            for _ in finishing:
                pass
            attention_done = [x1_in[B - 1], done, p_last] if (p_last := last) else []

        with ExitStack() as sc:
            W1 = sbuf("W1s", [P, E, FF], where=sc)
            W2 = sbuf("W2s", [P, E, NF, D], where=sc)
            x1T = sbuf("x1T", [P, 2, L], where=sc)
            lg = sbuf("lg", [P, TB, E], where=sc)
            t8 = sbuf("t8", [P, 4, TB, E], where=sc)
            t1 = sbuf("t1", [P, 6, TB], where=sc)
            comb = sbuf("comb", [P, 2, TB, E], where=sc)
            combT = sbuf("combT", [E, L], where=sc)
            hidden = Ring([Slot(sbuf(f"hidden{i}", [P, NF, L], where=sc)) for i in range(2)])
            moe = sbuf("moe", [P, 2, TB, D], where=sc)
            fin = sbuf("fin", [P, 2, TB, D], where=sc)
            stats = sbuf("stats_c", [P, 2, TB, 6], where=sc)
            mv = sbuf("mv_c", [P, 2, TB, 2], where=sc)
            rstd = sbuf("rstd_c", [P, 2, TB], where=sc)
            for e_ in range(E):
                moe_in = sp.dma(s_moe, W1[:, e_, :], a["W1"][e_], attention_done)
                moe_in = sp.dma(s_moe, W2[:, e_, :, :], a["W2"][e_].rearrange("(f p) d -> p f d", p=P), attention_done)
            x1T_free = [(), ()]
            comb_free = [(), ()]
            moe_free = [(), ()]
            route = {}
            misc = Ring(banks[0:2])
            up_banks = Ring(banks[2:6])
            down_banks = Ring(banks[6:8])
            small = ()
            def experts(b, small):
                s = b % 2
                X1b = X1[:, b * TB:(b + 1) * TB, :]
                bank = misc.take()
                turned = transpose_tiles(X1b, bank, [x1_in[b], *attention_done])
                x1T_in = dve.do(lambda e, k=bank: e.tensor_copy(x1T[:, s, :], k.ap), [turned, *x1T_free[s]])
                bank.free = (x1T_in,)
                bank = misc.take()
                for i in range(TB):
                    p_g = pe.do(lambda e, i=i, k=bank: e.matmul(k.ap[:, i * E:(i + 1) * E], x1T[:, s, i * P:(i + 1) * P], Wg[:, :], start=True, stop=True),
                                [x1T_in, *bank.free], signal=i == TB - 1)
                v = chain(dve)
                wide = lambda ap: ap.unsqueeze(2).to_broadcast([P, TB, E])
                erow = lambda r: r.unsqueeze(1).to_broadcast([P, TB, E])
                pr, mask, oh1, oh2 = (t8[:, n] for n in range(4))
                top, sm, rc, m1c, m2c, w1c = (t1[:, n] for n in range(6))
                m = v(lambda e, k=bank: e.tensor_tensor(lg[:, :, :], k.ap[:, 0:TB * E].rearrange("p (i e) -> p i e", e=E), erow(bg_row[:, :]), ALU.add), [p_g, *small])
                bank.free = (m,)
                v(lambda e: e.tensor_reduce(top, lg[:, :, :], AX.X, ALU.max))
                m = v(lambda e: e.tensor_tensor(lg[:, :, :], lg[:, :, :], wide(top), ALU.subtract))
                m = act.do(lambda e: e.activation(lg[:, :, :], lg[:, :, :], ACT.Exp), [m])
                v(lambda e: e.tensor_reduce(sm, lg[:, :, :], AX.X, ALU.add), [m])
                v(lambda e: e.reciprocal(rc, sm))
                v(lambda e: e.tensor_tensor(pr, lg[:, :, :], wide(rc), ALU.mult))
                for best, hot in ((m1c, oh1), (m2c, oh2)):
                    v(lambda e, best=best: e.tensor_reduce(best, pr, AX.X, ALU.max))
                    v(lambda e, best=best: e.tensor_tensor(mask, pr, wide(best), ALU.is_equal))
                    v(lambda e: e.tensor_tensor(mask, mask, erow(pri_row[:, :]), ALU.mult))
                    v(lambda e: e.tensor_reduce(w1c, mask, AX.X, ALU.max))
                    v(lambda e, hot=hot: e.tensor_tensor(hot, mask, wide(w1c), ALU.is_equal))
                    if hot is oh1:
                        v(lambda e: e.scalar_tensor_tensor(out=pr, in0=oh1, scalar=-2.0, in1=pr, op0=ALU.mult, op1=ALU.add))
                v(lambda e: e.scalar_tensor_tensor(out=pr, in0=oh1, scalar=2.0, in1=pr, op0=ALU.mult, op1=ALU.add))
                v(lambda e: e.tensor_tensor(oh1, oh1, oh2, ALU.add))
                v(lambda e: e.tensor_tensor(pr, pr, oh1, ALU.mult))
                v(lambda e: e.tensor_reduce(sm, pr, AX.X, ALU.add))
                v(lambda e: e.reciprocal(rc, sm))
                comb_in = v(lambda e: e.tensor_tensor(comb[:, s], pr, wide(rc), ALU.mult), comb_free[s])
                small = (comb_in,)
                bank = misc.take()
                for i in range(TB):
                    m = pe.do(lambda e, i=i, k=bank: e.transpose(k.ap[0:E, i * P:(i + 1) * P], comb[:, s, i, :], ident[:, :]), [comb_in, *bank.free], signal=i == TB - 1)
                combT_in = dve.do(lambda e, k=bank: e.tensor_copy(combT[:, :], k.ap[0:E, :]), [m, *route.get("combT", ())])
                bank.free = (combT_in,)
                bank = misc.take()
                for i in range(TB):
                    m = pe.do(lambda e, i=i, k=bank: e.matmul(k.ap[:, i * P:(i + 1) * P], combT[:, i * P:(i + 1) * P], b2m[:, :], start=True, stop=True),
                              [combT_in, *bank.free], signal=i == TB - 1)
                route["combT"] = (m,)
                acc = moe[:, s].rearrange("p i d -> p (i d)")
                m = dve.do(lambda e, k=bank: e.tensor_tensor(acc, X1b.rearrange("p i d -> p (i d)"), k.ap, ALU.add), [m, *moe_free[s]])
                bank.free = (m,)
                for e_ in range(E):
                    slot = hidden.take()
                    acts = []
                    for f in range(NF):
                        bank = up_banks.take()
                        p_u = pe.do(lambda e, e_=e_, f=f, k=bank: e.matmul(k.ap, W1[:, e_, f * P:(f + 1) * P], x1T[:, s, :], start=True, stop=True), [x1T_in, moe_in, *bank.free])
                        g_ = act.do(lambda e, e_=e_, f=f, k=bank, t=slot: e.activation(t.ap[:, f, :], k.ap, ACT.Gelu, bias=b1c[:, e_, f:f + 1]), [p_u, *slot.free])
                        bank.free = (g_,)
                    bank = down_banks.take()
                    for i in range(TB):
                        for f in range(NF):
                            p_d = pe.do(lambda e, e_=e_, i=i, f=f, k=bank, t=slot: e.matmul(
                                k.ap[:, i * P:(i + 1) * P], t.ap[:, f, i * P:(i + 1) * P], W2[:, e_, f, :], start=f == 0, stop=f == NF - 1),
                                [g_, *bank.free], signal=i == TB - 1 and f == NF - 1)
                    slot.free = (p_d,)
                    for i in range(TB):
                        m = dve.do(lambda e, e_=e_, i=i, k=bank: e.scalar_tensor_tensor(
                            out=moe[:, s, i, :], in0=k.ap[:, i * P:(i + 1) * P], scalar=comb[:, s, i, e_:e_ + 1], in1=moe[:, s, i, :],
                            op0=ALU.mult, op1=ALU.add), [p_d, m])
                    bank.free = (m,)
                x1T_free[s] = (p_u,)
                comb_free[s] = (m,)
                normed = normalise(moe[:, s], fin[:, s], stats[:, s], mv[:, s], rstd[:, s], [m], moe_free[s])
                v = chain(pool)
                v(lambda e: e.tensor_tensor(fin[:, s], fin[:, s], over_tiles(row("g2")), ALU.mult), [normed])
                v(lambda e: e.tensor_tensor(fin[:, s], fin[:, s], over_tiles(row("be2")), ALU.add))
                v(lambda e, b=b: e.tensor_tensor(fin[:, s], fin[:, s], over_tiles(rows[:, b, GB, :]), ALU.mult), rows_ready)
                m = v(lambda e, b=b: e.tensor_tensor(fin[:, s], fin[:, s], X[:, b * TB:(b + 1) * TB, :], ALU.add))
                stored = sp.dma((s_out0, s_out1)[s], out_tiles[b], fin[:, s], [m])
                moe_free[s] = (normed, stored)
                return stored, small

            for b in range(B):
                stored, small = experts(b, small)
            sp.wait((s_out0.sem, s_out0.count), (s_out1.sem, s_out1.count))

        block = scope.enter_context(nc.Block())

        @block.sync
        def _(engine):
            sp.play(engine)

        @block.scalar
        def _(engine):
            act.play(engine)

        @block.vector
        def _(engine):
            dve.play(engine)

        @block.gpsimd
        def _(engine):
            pool.play(engine)

        @block.tensor
        def _(engine):
            pe.play(engine)


def _layout(inputs):
    import numpy as np

    g = {k: np.asarray(v) for k, v in inputs.items()}
    B, L, D = g["L0_attn_x"].shape
    E, _, FF = g["L0_ffn_W1"].shape
    H, HD = 16, D // 16
    order = np.array([(4 * gg + G) * HD + d for gg in range(4) for d in range(HD) for G in range(4)])
    swap = np.array([(c // HD) * HD + (c % HD + HD // 2) % HD for c in range(D)])
    rot = swap[order]
    d_of = order % HD
    inv = 1.0 / 10000.0 ** (np.arange(0, HD, 2, dtype=np.float32) / np.float32(HD))
    freqs = (np.arange(L, dtype=np.float32)[:, None] * inv.astype(np.float32)[None, :]).astype(np.float32)
    emb = np.concatenate([freqs, freqs], -1)
    cos, sin = np.cos(emb).astype(np.float32), np.sin(emb).astype(np.float32)
    sign = np.where(d_of < HD // 2, -1.0, 1.0).astype(np.float32)
    c = np.ascontiguousarray
    Wi = g["L0_attn_W_in"]
    return {
        "x": c(g["L0_attn_x"]), "cT": c(g["L0_c"].T), "wmod": c(g["L0_wmod"]),
        "ident": np.eye(D, dtype=np.float32), "priority": np.arange(E, 0, -1).astype(np.float32),
        "W_in_u": c(Wi[:D]), "W_gateT": c(Wi[D:].T), "W_stateT": c(g["L0_attn_W_state"].T), "W_dtT": c(g["L0_attn_W_dt"].T),
        "W_CT": c(g["L0_attn_W_C"].T), "W_outT": c(g["L0_attn_W_out"].T),
        "b_dt": c(g["L0_attn_b_dt"]), "A_log": c(g["L0_attn_A_log"]), "Dskip": c(g["L0_attn_D"]),
        "Wq": c(g["L0_ffn_Wq"][:, order]), "Wq_rot": c(g["L0_ffn_Wq"][:, rot]), "bq": c(g["L0_ffn_bq"][order]), "bq_rot": c(g["L0_ffn_bq"][rot]),
        "Wk": c(g["L0_ffn_Wk"][:, order]), "Wk_rot": c(g["L0_ffn_Wk"][:, rot]), "bk": c(g["L0_ffn_bk"][order]), "bk_rot": c(g["L0_ffn_bk"][rot]),
        "Wv": c(g["L0_ffn_Wv"]), "Wo": c(g["L0_ffn_Wo"]), "bv": c(g["L0_ffn_bv"]), "bo": c(g["L0_ffn_bo"]),
        "cos": c(cos.T[d_of]), "sin": c(sin.T[d_of] * sign[:, None]),
        "g1": c(g["L0_ffn_g1"]), "be1": c(g["L0_ffn_be1"]), "g2": c(g["L0_ffn_g2"]), "be2": c(g["L0_ffn_be2"]),
        "Wg": c(g["L0_ffn_Wg"]), "bg": c(g["L0_ffn_bg"]), "W1": c(g["L0_ffn_W1"]), "W2": c(g["L0_ffn_W2"]),
        "b1T": c(g["L0_ffn_b1"].reshape(E, FF // 128, 128).transpose(2, 0, 1)), "b2": c(g["L0_ffn_b2"]),
    }


def kernel(**inputs):
    import concourse.bacc as _bacc
    from concourse import mybir as _mybir
    from concourse.bass_utils import run_bass_kernel_spmd as _run

    arrays = _layout(inputs)
    nc = _bacc.Bacc("TRN2", target_bir_lowering=False, num_devices=1)
    aps = {k: nc.dram_tensor(f"in_{k}", v.shape, _mybir.dt.from_np(v.dtype), kind="ExternalInput").ap() for k, v in arrays.items()}
    out = nc.dram_tensor("out_0", arrays["x"].shape, _mybir.dt.float32, kind="ExternalOutput").ap()
    adaln_block(nc, aps, out)
    r = _run(nc, [{f"in_{k}": v for k, v in arrays.items()}], core_ids=[0])
    return r.results[0]["out_0"]
```

```python
from contextlib import ExitStack

import concourse.bass as bass
from concourse import mybir

ALU = mybir.AluOpType
ACT = mybir.ActivationFunctionType
AX = mybir.AxisListType
F32 = mybir.dt.float32
F32R = mybir.dt.float32r
I32 = mybir.dt.int32

P = 128
LN_EPS = 1e-5
RATE_EPS = 1e-4
DT_MAX = 10.0
DT_CLAMP = 20.0
MIN_GATE = 0.25
BANK = 512
SMAX_BANKS = 3
PV_AT = 1


class Queue:

    def __init__(self, sem):
        self.sem, self.count, self.steps, self.met = sem, 0, [], {}

    def wait(self, *marks):
        for sem, value in marks:
            if self.met.get(sem.name, 0) < value:
                self.met[sem.name] = value
                self.steps.append(lambda e, s=sem, v=value: e.wait_ge(s, v))

    def do(self, instruction, after=(), signal=True):
        self.wait(*after)
        if not signal:
            self.steps.append(instruction)
            return None
        self.count += 1
        self.steps.append(lambda e: instruction(e).then_inc(self.sem, 1))
        return (self.sem, self.count)

    def dma(self, stream, out, in_, after=()):
        self.wait(*after)
        stream.count += 16
        self.steps.append(lambda e: e.dma_start(out, in_).then_inc(stream.sem, 16))
        return (stream.sem, stream.count)

    def play(self, engine):
        for step in self.steps:
            step(engine)


class Stream:

    def __init__(self, sem):
        self.sem, self.count = sem, 0


class Slot:

    def __init__(self, ap):
        self.ap, self.marks, self.held = ap, (), False

    @property
    def free(self):
        return self.marks

    @free.setter
    def free(self, marks):
        self.marks, self.held = tuple(marks), False


class Ring:

    def __init__(self, slots):
        self.slots, self.n = slots, 0

    def ready(self):
        return not all(slot.held for slot in self.slots)

    def take(self):
        assert self.ready(), "all slots taken"
        while self.slots[self.n % len(self.slots)].held:
            self.n += 1
        slot = self.slots[self.n % len(self.slots)]
        self.n += 1
        slot.held = True
        return slot

    def get(self):
        while not self.ready():
            yield
        return self.take()


class Region:

    def __init__(self, nc, start):
        self.nc, self.at = nc, start

    def place(self, name, shape, dtype=F32):
        size = 4
        for n in shape[1:]:
            size *= n
        start = (self.at + 31) // 32 * 32
        self.at = start + size
        assert self.at <= self.nc.sbuf_usable_end, (name, self.at)
        return self.nc.alloc_sbuf_tensor_at(name, shape, dtype, offset=start)


def run_beside(parts, at_once):
    running, parts = [], list(parts)
    while parts or running:
        if parts and len(running) < at_once:
            running.append(parts.pop(0))
        for part in list(running):
            if next(part, "ended") == "ended":
                running.remove(part)


def adaln_block(nc, a, out):
    B, L, D = a["x"].shape
    TB = L // P
    NT = B * TB
    H = 16
    HD = D // H
    G4 = 4
    E, _, FF = a["W1"].shape
    NF = FF // P
    K = 2
    SCORE_SCALE = float(HD) ** -0.5
    DEEP = 3
    LEAD = 24
    GROUPS = ((0, B - 2), (B - 2, B))
    assert D == P and L == BANK and H == G4 * G4 and 3 * HD < 32
    tiles_of = [(K * L * (hi - lo) + E * (P - 1)) // P for lo, hi in GROUPS]

    x_tiles = a["x"].rearrange("b (i p) d -> b p i d", p=P)
    out_tiles = out.rearrange("b (i p) d -> b p i d", p=P)
    sorted_x = [nc.dram_tensor(f"sorted_x{n}", [t * P, D], F32).ap() for n, t in enumerate(tiles_of)]
    sorted_y = [nc.dram_tensor(f"sorted_y{n}", [t * P, D], F32).ap() for n, t in enumerate(tiles_of)]

    with ExitStack() as scope:
        sem = lambda name: scope.enter_context(nc.semaphore(name))
        pe, act, dve, pool, sp = (Queue(sem(n)) for n in ("pe_done", "act_done", "dve_done", "pool_done", "sp_done"))
        stream = lambda name: Stream(sem(name))
        s_first, s_weights, s_zero, s_moe = stream("first_in"), stream("weights_in"), stream("zeroed"), stream("moe_weights_in")
        s_ones = stream("ones_row_in")
        s_x = [stream(f"x_in_{b}") for b in range(B)]
        s_stack = [stream(f"stack_in_{n}") for n in range(2)]
        s_max = [stream(f"max_in_{n}") for n in range(4)]
        s_scatter = [stream(f"scattered_{n}") for n in range(2)]
        s_load = [stream(f"sorted_x_in_{n}") for n in range(4)]
        s_store = [stream(f"sorted_y_out_{n}") for n in range(4)]
        s_gather = [stream(f"gathered_{n}") for n in range(2)]
        s_out = [stream(f"out_stored_{n}") for n in range(2)]
        psum = scope.enter_context(nc.psum_tensor("psum", [P, 8, BANK], F32))
        banks = [Slot(psum[:, n, :]) for n in range(8)]

        keep = Region(nc, nc.sbuf_base)
        X = keep.place("X", [P, NT, D])
        ident = keep.place("ident", [P, P])
        rows = keep.place("rows", [P, B, 4, D])
        SB, CB, GG, GBE = range(4)
        vec_names = ["b_dt", "A_log", "Dskip", "bq", "bq_rot", "bk", "bk_rot", "bv"]
        vecs = keep.place("vecs", [P, len(vec_names)])
        row_names = ["bo", "g1", "be1", "g2", "be2"]
        rowc = keep.place("rowc", [P, len(row_names), D])
        bg_row = keep.place("bg_row", [P, E])
        pri_row = keep.place("pri_row", [P, E])
        b1c = keep.place("b1c", [P, E, NF])
        Wg = keep.place("Wg_sb", [P, E])
        Wqkv = keep.place("Wqkv", [P, 6, D])
        W_Q, W_QR, W_K, W_KR, W_V, W_O = range(6)
        cos_t = keep.place("cos_t", [P, L])
        sin_t = keep.place("sin_t", [P, L])
        modc = keep.place("modc", [P, 2, B])
        negrate = keep.place("negrate", [P, 1])
        half = keep.place("half", [P, TB])
        attn_row = keep.place("attn_row", [P, D])
        ones = keep.place("ones", [P, P])
        before = keep.place("before_sb", [P, P])
        tile_no = keep.place("tile_no_sb", [1, max(tiles_of)])
        hot = [keep.place(f"hot{k}", [P, E, NT]) for k in range(K)]
        share = [keep.place(f"share{k}", [P, NT]) for k in range(K)]
        slot_of = [keep.place(f"slot_of{k}", [P, NT], I32) for k in range(K)]
        expert_of = [keep.place(f"expert_of{n}", [1, t], I32) for n, t in enumerate(tiles_of)]
        hT = Region(nc, keep.at).place("hT", [P, B, L])
        X1 = keep.place("X1", [P, NT, D])
        assert B * L == NT * D
        b2_at = keep.at
        QS, KS = [None, None], [None, None]
        KS[0] = keep.place("KS0", [P, G4, L], F32R)
        experts_at = keep.at
        QS[0] = keep.place("QS0", [P, H, L], F32R)
        late_at = keep.at
        KS[1] = keep.place("KS1", [P, G4, L], F32R)
        QS[1] = keep.place("QS1", [P, H, L], F32R)
        rest_at = keep.at

        ssm = Region(nc, rest_at)
        gate = ssm.place("gate", [P, B, L])
        Wssm = ssm.place("Wssm", [P, 6, D])
        W_INU, W_GATE, W_STATE, W_DT, W_C, W_OUT = range(6)
        Wfused = ssm.place("Wfused", [P, 2, D])
        Wout_b = ssm.place("Wout_b", [P, B, D])
        rate3 = ssm.place("rate3", [P, 3])
        stats_a = ssm.place("stats_a", [P, DEEP, TB, 6])
        mv_a = ssm.place("mv_a", [P, DEEP, TB, 2])
        rstd_a = ssm.place("rstd_a", [P, DEEP, TB])
        xn_a = ssm.place("xn_a", [P, DEEP, TB, D])
        ssm_work = [{n: ssm.place(f"{n}_{i}", [P, L]) for n in ("dt", "ed", "drive", "z")} for i in range(DEEP)]

        setup = Region(nc, late_at)
        wmod = setup.place("wmod_sb", [P, 6, D])
        cT = setup.place("cT_sb", [P, B])
        silu_c = setup.place("silu_c", [P, B])
        silu_cb = setup.place("silu_cb", [P, B, P])
        bv_b = setup.place("bv_b", [P, P])
        gates = setup.place("gates", [P, 2, B, D])
        gsign = setup.place("gsign", [P, 2, B, D])
        zeros = setup.place("zeros", [P, 8 * D])

        col = lambda name: vecs[:, vec_names.index(name):vec_names.index(name) + 1]
        row = lambda name: rowc[:, row_names.index(name), :]
        over_tiles = lambda ap: ap.unsqueeze(1).to_broadcast([P, TB, D])
        tiles = lambda t, b: t[:, b * TB:(b + 1) * TB, :]
        flat = lambda ap: ap.rearrange("p i d -> p (i d)")

        sp.dma(s_first, cT[:, :], a["cT"])
        x_in = [sp.dma(s_x[0], tiles(X, 0), x_tiles[0])]
        act.dma(s_first, wmod[:, :, :], a["wmod"].rearrange("c (n d) -> c n d", n=6))
        first_in = act.dma(s_first, ident[:, :], a["ident"])
        w = s_weights
        for n, name in enumerate(("W_in_u", "W_gateT", "W_stateT", "W_dtT", "W_CT", "W_outT")):
            sp.dma(w, Wssm[:, n, :], a[name])
        sp.dma(w, vecs[:, :], a["vecs"])
        x_in += [sp.dma(s_x[b], tiles(X, b), x_tiles[b]) for b in range(1, B)]
        for n, name in enumerate(("Wq", "Wq_rot", "Wk", "Wk_rot", "Wv", "Wo")):
            sp.dma(w, Wqkv[:, n, :], a[name])
        for n, name in enumerate(row_names):
            sp.dma(w, rowc[:, n, :], a[name].partition_broadcast(P))
        sp.dma(w, bg_row[:, :], a["bg"].partition_broadcast(P))
        sp.dma(w, pri_row[:, :], a["priority"].partition_broadcast(P))
        sp.dma(w, b1c[:, :, :], a["b1T"])
        sp.dma(w, Wg[:, :], a["Wg"])
        sp.dma(w, cos_t[:, :], a["cos"])
        sp.dma(w, before[:, :], a["before"])
        sp.dma(w, tile_no[:, :], a["tile_no"])
        weights_in = sp.dma(w, sin_t[:, :], a["sin"])

        half_set = dve.do(lambda e: e.memset(half[:, :], -0.5))
        ones_set = dve.do(lambda e: e.memset(ones[:, :], 1.0))
        zeros_set = pool.do(lambda e: e.memset(zeros[:, :], 0.0))
        for n, t in enumerate(tiles_of):
            for t0 in range(0, t, 8):
                m = min(8, t - t0)
                zeroed = sp.dma(s_zero, sorted_x[n][t0 * P:(t0 + m) * P, :].rearrange("(p i) d -> p i d", p=P),
                                zeros[:, 0:m * D].rearrange("p (i d) -> p i d", d=D), [zeros_set])

        def chain(queue):
            last = [()]

            def step(instruction, after=()):
                mark = queue.do(instruction, [*last[0], *after])
                last[0] = (mark,)
                return mark
            return step

        def normalise(src, dst, stats, mv, rstd, after, free):
            for i in range(TB):
                seen = dve.do(lambda e, i=i: e.bn_stats(stats[:, i, :], src[:, i, :]), [*after, *free])
            for i in range(TB):
                summed = dve.do(lambda e, i=i: e.bn_aggr(mv[:, i, :], stats[:, i, :]), [seen])
            with_eps = pool.do(lambda e: e.tensor_scalar(rstd[:, :], mv[:, :, 1], LN_EPS, None, ALU.add), [summed])
            powered = pool.do(lambda e: e.tensor_tensor(rstd[:, :], rstd[:, :], half[:, :], ALU.pow), [with_eps, half_set])
            yield
            yield
            yield
            for i in range(TB):
                done = dve.do(lambda e, i=i: e.tensor_scalar(
                    dst[:, i, :], src[:, i, :], mv[:, i, 0:1], rstd[:, i:i + 1], ALU.subtract, ALU.mult), [powered])
            return done

        def transpose_tiles(src, bank, after):
            for i in range(TB):
                done = pe.do(lambda e, i=i: e.transpose(bank.ap[:, i * P:(i + 1) * P], src(i), ident[:, :]),
                             [*after, *bank.free], signal=i == TB - 1)
            return done

        def per_tile_product(bank, lhsT, rhs, after, width=D):
            for i in range(TB):
                done = pe.do(lambda e, i=i: e.matmul(bank.ap[:, i * width:(i + 1) * width], lhsT(i), rhs, start=True, stop=True),
                             [*after, *bank.free], signal=i == TB - 1)
            return done

        silued = act.do(lambda e: e.activation(silu_c[:, :], cT[:, :], ACT.Silu), [first_in])
        for n in range(2):
            mods = pe.do(lambda e, n=n: e.matmul(banks[0].ap[:, n * B:(n + 1) * B], wmod[:, n, :], silu_c[:, :], start=True, stop=True), [silued])
        mod_sa = dve.do(lambda e: e.tensor_copy(modc[:, 0, :], banks[0].ap[:, 0:B]), [mods])
        mod_ready = dve.do(lambda e: e.tensor_scalar(modc[:, 1, :], banks[0].ap[:, B:2 * B], 1.0, None, ALU.add), [mods])
        banks[0].free = (mod_sa, mod_ready)
        made_ready = {}

        def make_rows():
            for b in range(B):
                spread = dve.do(lambda e, b=b: e.tensor_scalar(silu_cb[:, b, :], ones[:, :], silu_c[:, b:b + 1], None, ALU.mult), [silued, ones_set])
            bv_spread = dve.do(lambda e: e.tensor_scalar(bv_b[:, :], ones[:, :], col("bv"), None, ALU.mult), [weights_in, ones_set])
            yield
            for b in range(B):
                bank = banks[6 + b % 2]
                made = pe.do(lambda e, b=b, k=bank: e.matmul(k.ap, silu_cb[:, b, :], wmod[:, 2:6, :].rearrange("c n d -> c (n d)"),
                                                            start=True, stop=True), [spread, *bank.free])
                sb_cb = act.do(lambda e, b=b, k=bank: e.activation(rows[:, b, SB:CB + 1, :], k.ap[:, D:3 * D].rearrange("p (n d) -> p n d", n=2), ACT.Copy), [made])
                ga_in = act.do(lambda e, b=b, k=bank: e.activation(gates[:, 0, b, :], k.ap[:, 0:D], ACT.Copy), [made])
                gb_in = act.do(lambda e, b=b, k=bank: e.activation(gates[:, 1, b, :], k.ap[:, 3 * D:4 * D], ACT.Copy), [made])
                bank.free = (gb_in, ga_in, sb_cb)
                yield
            g, sgn = gates[:, :, :, :].rearrange("p n b d -> p (n b d)"), gsign[:, :, :, :].rearrange("p n b d -> p (n b d)")
            signed = dve.do(lambda e: e.tensor_scalar(sgn, g, 0.0, 2.0, ALU.is_ge, ALU.mult), [ga_in, gb_in])
            yield
            m = dve.do(lambda e: e.scalar_tensor_tensor(out=g, in0=g, scalar=-1.0, in1=g, op0=ALU.mult, op1=ALU.max), [signed])
            yield
            m = dve.do(lambda e: e.tensor_scalar(g, g, MIN_GATE, None, ALU.max), [m])
            yield
            m = dve.do(lambda e: e.scalar_tensor_tensor(out=g, in0=sgn, scalar=-1.0, in1=g, op0=ALU.add, op1=ALU.mult), [m])
            gates_ready = m
            yield
            made_ready["cb"] = pool.do(lambda e: e.tensor_scalar(rows[:, :, CB, :], rows[:, :, CB, :], 1.0, 1.0, ALU.add, ALU.mult), [sb_cb])
            over_rows = lambda ap: ap.unsqueeze(1).to_broadcast([P, B, D])
            made_ready["Wout"] = dve.do(lambda e: e.tensor_tensor(Wout_b[:, :, :], gates[:, 0, :, :], over_rows(Wssm[:, W_OUT, :]), ALU.mult), [gates_ready, weights_in])
            yield
            gg = pool.do(lambda e: e.tensor_tensor(rows[:, :, GG, :], gates[:, 1, :, :], over_rows(row("g2")), ALU.mult), [gates_ready, weights_in, gb_in])
            made_ready["gg"] = pool.do(lambda e: e.tensor_tensor(rows[:, :, GBE, :], gates[:, 1, :, :], over_rows(row("be2")), ALU.mult), [gg])
            row_bank = banks[7]
            bv_wo = pe.do(lambda e: e.matmul(row_bank.ap[:, 0:D], bv_b[:, :], Wqkv[:, W_O, :], start=True, stop=True), [bv_spread, *row_bank.free])
            made_ready["attn_row"] = dve.do(lambda e: e.tensor_tensor(attn_row[:, :], row_bank.ap[:, 0:D], row("bo"), ALU.add), [bv_wo])
            row_bank.free = (made_ready["attn_row"],)
            yield
            fused_bank = banks[6]
            for n, wi in enumerate((W_STATE, W_DT)):
                fused = pe.do(lambda e, n=n, wi=wi: e.matmul(fused_bank.ap[:, n * D:(n + 1) * D], Wssm[:, W_INU, :], Wssm[:, wi, :], start=True, stop=True), [weights_in, *fused_bank.free])
            made_ready["fused"] = dve.do(lambda e: e.tensor_copy(Wfused[:, :, :].rearrange("p n d -> p (n d)"), fused_bank.ap[:, 0:2 * D]), [fused])
            fused_bank.free = (made_ready["fused"],)
            m = dve.do(lambda e: e.scalar_tensor_tensor(out=rate3[:, 0:1], in0=col("A_log"), scalar=-1.0, in1=col("A_log"), op0=ALU.mult, op1=ALU.min), [weights_in])
            made_ready["A"] = dve.do(lambda e: e.tensor_scalar(rate3[:, 1:2], col("A_log"), 0.0, None, ALU.max), [m])
            yield
            setup_read = [zeroed, made, mods, bv_wo, made_ready["Wout"], made_ready["gg"]]
            cleared = []
            for t in (QS[0], KS[0], QS[1], KS[1]):
                width = t.shape[1]
                for j in range(0, width, 4):
                    cleared.append(pool.do(lambda e, t=t, j=j: e.memset(t[:, j:j + 4, :].bitcast(F32), 0.0), setup_read if t in (QS[1], KS[1]) else ()))
                    yield
            made_ready["cleared"] = [cleared[-1]]

        hT_in, gated, x2_in = {}, {}, {}
        a_free = [() for _ in range(DEEP)]
        turn_banks, gate_banks = Ring(banks[0:3]), Ring(banks[3:6])

        def first_part(b):
            s = b % DEEP
            xn = xn_a[:, s]
            normed = yield from normalise(tiles(X, b), xn, stats_a[:, s], mv_a[:, s], rstd_a[:, s], [x_in[b]], a_free[s])
            yield
            bank = turn_banks.take()
            turned = transpose_tiles(lambda i: xn[:, i, :], bank, [normed, first_in])
            a_free[s] = (turned,)
            yield
            hT_in[b] = act.do(lambda e: e.activation(hT[:, b, :], bank.ap, ACT.Identity, bias=modc[:, 0, b:b + 1], scale=modc[:, 1, b:b + 1]),
                              [turned, mod_sa, mod_ready])
            bank.free = (hT_in[b],)
            yield
            out_bank = gate_banks.take()
            product = pe.do(lambda e: e.matmul(out_bank.ap, Wssm[:, W_GATE, :], hT[:, b, :], start=True, stop=True), [hT_in[b], weights_in, *out_bank.free])
            yield
            gated[b] = act.do(lambda e: e.activation(gate[:, b, :], out_bank.ap, ACT.Silu), [product])
            out_bank.free = (gated[b],)

        run_beside([make_rows()] + [first_part(b) for b in range(B)], DEEP + 1)
        rows_ready = [made_ready["cb"]]

        act.steps.append(lambda e: e.preload_act_table_set("natural_log_exp_and_others"))
        m = act.do(lambda e: e.activation(rate3[:, 2:3], rate3[:, 0:1], ACT.Exp), [made_ready["A"]])
        m = act.do(lambda e: e.activation(rate3[:, 2:3], rate3[:, 2:3], ACT.Ln, bias=1.0), [m])
        m = dve.do(lambda e: e.tensor_tensor(rate3[:, 2:3], rate3[:, 2:3], rate3[:, 1:2], ALU.add), [m])
        rate_ready = dve.do(lambda e: e.tensor_scalar(negrate[:, :], rate3[:, 2:3], RATE_EPS, -1.0, ALU.add, ALU.mult), [m])
        ssm_free = [{n: () for n in w} for w in ssm_work]
        for bank in banks:
            bank.free = tuple(m for k in banks for m in k.free)
        dt_banks, b_banks, y_banks, o_banks = (Ring(banks[n:n + 2]) for n in (0, 2, 4, 6))
        ssm_ends = []

        def second_part(b):
            s = b % DEEP
            dt, ed, drive, z = (ssm_work[s][n] for n in ("dt", "ed", "drive", "z"))
            free = ssm_free[s]
            bank_dt = dt_banks.take()
            p_dt = pe.do(lambda e: e.matmul(bank_dt.ap, Wfused[:, 1, :], hT[:, b, :], start=True, stop=True), [hT_in[b], made_ready["fused"], *bank_dt.free])
            yield
            m = dve.do(lambda e: e.tensor_scalar(dt[:, :], bank_dt.ap, col("b_dt"), DT_CLAMP, ALU.add, ALU.min), [p_dt, *free["dt"]])
            bank_dt.free = (m,)
            yield
            m = act.do(lambda e: e.activation(ed[:, :], dt[:, :], ACT.Exp), [m, *free["ed"]])
            m = act.do(lambda e: e.activation(dt[:, :], ed[:, :], ACT.Ln, bias=1.0), [m])
            yield
            m = pool.do(lambda e: e.tensor_scalar(ed[:, :], dt[:, :], DT_MAX, negrate[:, 0:1], ALU.min, ALU.mult), [m, rate_ready])
            free["dt"] = (m,)
            yield
            m = act.do(lambda e: e.activation(ed[:, :], ed[:, :], ACT.Exp), [m])
            bank_b = b_banks.take()
            p_b = pe.do(lambda e: e.matmul(bank_b.ap, Wfused[:, 0, :], hT[:, b, :], start=True, stop=True), [*bank_b.free])
            yield
            m = dve.do(lambda e: e.tensor_scalar(ed[:, :], ed[:, :], 0.0, 1.0, ALU.max, ALU.min), [m])
            m = dve.do(lambda e: e.scalar_tensor_tensor(out=drive[:, :], in0=ed[:, :], scalar=-1.0, in1=bank_b.ap, op0=ALU.add, op1=ALU.mult), [m, p_b, *free["drive"]])
            bank_b.free = (m,)
            yield
            m = dve.do(lambda e: e.tensor_tensor_scan(dt[:, :], ed[:, :], drive[:, :], 0.0, ALU.mult, ALU.subtract), [m, *free["dt"]])
            free["ed"] = free["drive"] = (m,)
            yield
            bank_y = y_banks.take()
            p_y = pe.do(lambda e: e.matmul(bank_y.ap, Wssm[:, W_C, :], dt[:, :], start=True, stop=True), [m, *bank_y.free])
            free["dt"] = (p_y,)
            yield
            m = dve.do(lambda e: e.tensor_tensor(z[:, :], bank_y.ap, gate[:, b, :], ALU.mult), [p_y, gated[b], *free["z"]])
            bank_y.free = (m,)
            yield
            m = dve.do(lambda e: e.scalar_tensor_tensor(out=z[:, :], in0=hT[:, b, :], scalar=col("Dskip"), in1=z[:, :], op0=ALU.mult, op1=ALU.add), [m])
            yield
            bank_o = o_banks.take()
            p_o = per_tile_product(bank_o, lambda i: z[:, i * P:(i + 1) * P], Wout_b[:, b, :], [m, made_ready["Wout"]])
            free["z"] = (p_o,)
            yield
            x2_in[b] = dve.do(lambda e: e.tensor_tensor(flat(tiles(X, b)), flat(tiles(X, b)), bank_o.ap, ALU.add), [p_o])
            bank_o.free = (x2_in[b],)
            ssm_ends[:] = [x2_in[b], p_o]

        run_beside([second_part(b) for b in range(B)], DEEP)
        ssm_done = list(ssm_ends)
        ssm_done.append((pool.sem, pool.count))
        ssm_done.append((act.sem, act.count))
        for bank in banks:
            bank.free = (*ssm_done,)

        HI1, HI2, LO, MAXROW = 0, HD, 2 * HD, 3 * HD
        VW = 32
        mid = Region(nc, rest_at)
        vaug = [mid.place(f"vaug{i}", [P, TB, H, VW]) for i in range(2)]
        PT = Ring([Slot(mid.place(f"PT{i}", [P, L])) for i in range(8)])
        h2 = mid.place("h2", [P, 3, TB, D])
        turned_x = Ring([Slot(mid.place(f"turned_x{i}", [P, L])) for i in range(2)])
        h2T_slot = Slot(mid.place("h2T", [P, L]))
        rope = [mid.place(f"rope{i}", [P, L]) for i in range(2)]
        hi = mid.place("hi", [P, L], F32R)
        lo = mid.place("lo", [P, L], F32R)
        negmax = mid.place("negmax", [P, 2, G4 * TB])
        maxT = mid.place("maxT", [G4 * TB, 2, P], F32R)
        oT = mid.place("oT", [P, L])
        rsum = mid.place("rsum", [P, TB, G4])
        ao = mid.place("ao", [P, 2, TB, D])
        stats_b = mid.place("stats_b", [P, 2, TB, 6])
        mv_b = mid.place("mv_b", [P, 2, TB, 2])
        rstd_b = mid.place("rstd_b", [P, 2, TB])
        constrow = mid.place("constrow", [G4 * TB, 2, P])
        lg = mid.place("lg", [P, TB, E])
        t8 = mid.place("t8", [P, 2, TB, E])
        t1 = mid.place("t1", [P, 6, TB])
        NTG = max(h - l for l, h in GROUPS) * TB
        sorting = Region(nc, mid.at)
        counts = sorting.place("counts", [P, E * NTG])
        running = sorting.place("running", [P, E * NTG])
        e8 = sorting.place("e8", [P, 5, E])
        e8i = sorting.place("e8i", [P, E], I32)
        picks = sorting.place("picks", [P, NTG])
        compared = sorting.place("compared", [1, max(tiles_of), E])
        tile_expert = sorting.place("tile_expert", [1, max(tiles_of)])

        cleared = [*made_ready["cleared"]]
        row_set = [dve.do(lambda e: e.memset(constrow[:, 0, :], 0.0), ssm_done), dve.do(lambda e: e.memset(constrow[:, 1, :], 1.0), ssm_done)]
        for i in range(2):
            for g in range(G4):
                r = 32 * g + MAXROW
                ones_in = sp.dma(s_ones, KS[i][r:r + 1, :, :].bitcast(F32), constrow[:, 1, :], [*row_set, *cleared])
        v_ones = pool.do(lambda e: e.memset(vaug[0][:, :, :, HD:VW], 0.0), ssm_done)
        v_ones = pool.do(lambda e: e.memset(vaug[0][:, :, :, HD:HD + 1], 1.0), [v_ones])
        v_set = [(v_ones,), None]

        smax_banks, score_banks = Ring(banks[0:SMAX_BANKS]), Ring(banks[SMAX_BANKS:5])
        pv_banks, misc = Ring(banks[5:6]), Ring(banks[6:8])
        stack_read = [(), ()]
        v_read = [(), ()]
        h2_free = [(), (), ()]
        held = {k: () for k in ("hi", "lo", "max0", "max1", "oT", "ao0", "ao1", "rs", "rope0", "rope1", "small", "slots")}
        ready, sent, x1_in, routed = {}, {}, {}, {}

        def prepare(b):
            s, hs = b % 2, h2[:, b % 3]
            if b == 1:
                v_ones = pool.do(lambda e: e.memset(vaug[1][:, :, :, HD:VW], 0.0), ssm_done)
                v_ones = pool.do(lambda e: e.memset(vaug[1][:, :, :, HD:HD + 1], 1.0), [v_ones])
                v_set[1] = (v_ones,)
            normed = yield from normalise(tiles(X, b), hs, stats_b[:, 0], mv_b[:, 0], rstd_b[:, 0], [x2_in[b], *ssm_done], h2_free[b % 3])
            m = pool.do(lambda e: e.tensor_tensor(hs, hs, over_tiles(rows[:, b, CB, :]), ALU.mult), [normed, *rows_ready])
            yield
            h2_in = pool.do(lambda e: e.tensor_tensor(hs, hs, over_tiles(rows[:, b, SB, :]), ALU.add), [m])
            yield
            yield
            yield
            bank, slot = (yield from misc.get()), h2T_slot
            turned = transpose_tiles(lambda i: hs[:, i, :], bank, [h2_in])
            h2T = slot.ap
            h2T_in = act.do(lambda e: e.activation(h2T[:, :], bank.ap, ACT.Copy), [turned, *slot.free])
            bank.free = (h2T_in,)
            yield
            yield
            for n, (wp, wr, bp, br) in enumerate(((W_Q, W_QR, "bq", "bq_rot"), (W_K, W_KR, "bk", "bk_rot"))):
                def rope_half(j, w_, bias, table):
                    bank = yield from misc.get()
                    p = pe.do(lambda e: e.matmul(bank.ap, Wqkv[:, w_, :], h2T[:, :], start=True, stop=True), [h2T_in, *bank.free])
                    m = dve.do(lambda e: e.scalar_tensor_tensor(out=rope[j][:, :], in0=bank.ap, scalar=col(bias), in1=table[:, :],
                                                                op0=ALU.add, op1=ALU.mult), [p, *held[f"rope{j}"]])
                    bank.free = (m,)
                    return m
                m1 = yield from rope_half(0, wp, bp, cos_t)
                yield
                yield
                m2 = yield from rope_half(1, wr, br, sin_t)
                yield
                yield
                m3 = pool.do(lambda e: e.tensor_tensor(rope[0][:, :], rope[0][:, :], rope[1][:, :], ALU.add), [m1, m2])
                held["rope1"] = (m3,)
                yield
                yield
                m4 = dve.do(lambda e: e.tensor_copy(hi[:, :], rope[0][:, :]), [m3, *held["hi"]])
                yield
                m5 = pool.do(lambda e: e.tensor_tensor(lo[:, :], rope[0][:, :], hi[:, :].bitcast(F32), ALU.subtract), [m4, *held["lo"]])
                held["rope0"] = (m5,)
                yield
                rows_of = ((HI1, hi), (HI2, hi), (LO, lo)) if n == 0 else ((HI1, hi), (LO, hi), (HI2, lo))
                if n == 0:
                    for g in range(G4):
                        r = 32 * g + MAXROW
                        sp.dma(s_stack[s], QS[s][r:r + 1, g * G4:(g + 1) * G4, :].bitcast(F32), constrow[:, 0, :], [*row_set, *cleared, *stack_read[s]])
                for r, part in rows_of:
                    for g in range(G4):
                        r0 = 32 * g + r
                        dst = QS[s][r0:r0 + HD, g * G4:(g + 1) * G4, :] if n == 0 else KS[s][r0:r0 + HD, :, :]
                        stacked = sp.dma(s_stack[s], dst.bitcast(F32), part[32 * g:32 * g + 32, :].bitcast(F32),
                                         [m4 if part is hi else m5, *cleared, *stack_read[s]])
                held["hi"] = held["lo"] = (stacked,)
                yield
            v_bank = yield from misc.get()
            p_v = per_tile_product(v_bank, lambda i: h2T[:, i * P:(i + 1) * P], Wqkv[:, W_V, :], [h2T_in])
            slot.free = (p_v,)
            yield
            v_in = act.do(lambda e: e.activation(vaug[s][:, :, :, 0:HD], v_bank.ap.rearrange("p (i h d) -> p i h d", i=TB, h=H), ACT.Copy), [p_v, *v_set[s], *v_read[s]])
            v_bank.free = (v_in,)
            ready[b] = (stacked, v_in, h2_in)
            yield

        def maxima():
            pending = []
            for n, (b, g) in enumerate(units):
                s, t = b % 2, n % 2
                assert b in ready, "the stacks of a batch row come before its maxima"
                for G in range(G4):
                    h = g * G4 + G
                    for i in range(TB):
                        bank = smax_banks.take()
                        p_s = pe.do(lambda e, G=G, h=h, i=i, k=bank, s=s: e.matmul(k.ap, QS[s][:, h, i * P:(i + 1) * P], KS[s][:, G, :], start=True, stop=True),
                                    [ready[b][0], ones_in, *bank.free])
                        found = dve.do(lambda e, c=G * TB + i, k=bank, t=t: e.tensor_reduce(negmax[:, t, c:c + 1], k.ap, AX.X, ALU.max, negate=True), [p_s, *held[f"max{t}"]])
                        bank.free = (found,)
                        if pending and G * TB + i >= 1 and (pending[0][0] or misc.ready()):
                            pending.pop(0)[1]()
                        yield
                state = {}

                def turn(t=t, found=found, state=state):
                    bank = state["bank"] = misc.take()
                    state["turned"] = pe.do(lambda e: e.transpose(bank.ap[0:G4 * TB, 0:P], negmax[:, t, :], ident[:, :]), [found, *bank.free])
                    m = dve.do(lambda e: e.tensor_copy(maxT[:, t, :], bank.ap[0:G4 * TB, 0:P]), [state["turned"], *held[f"max{t}"]])
                    bank.free = (m,)
                    state["m"] = m

                def send(n=n, b=b, g=g, s=s, t=t, state=state, last=p_s):
                    r = 32 * g + MAXROW
                    sent[n] = sp.dma(s_max[n % 4], QS[s][r:r + 1, g * G4:(g + 1) * G4, :].bitcast(F32), maxT[:, t, :].bitcast(F32), [state["m"], last])
                    held[f"max{t}"] = (sent[n],)
                pending = [(False, turn), (True, send)]
            while pending:
                if pending[0][0] or misc.ready():
                    pending.pop(0)[1]()
                yield

        def collect(b, g, t_in):
            bank = yield from misc.get()
            turned = transpose_tiles(lambda i: oT[:, i * P:(i + 1) * P], bank, [t_in])
            held["oT"] = (turned,)
            o = bank.ap.rearrange("p (i j r) -> p i j r", i=TB, j=G4)
            yield
            m = dve.do(lambda e: e.reciprocal(rsum[:, :, :].unsqueeze(3), o[:, :, :, HD:HD + 1]), [turned, *held["rs"]])
            dst = ao[:, b % 2, :, 32 * g:32 * g + 32].rearrange("p i (j d) -> p i j d", j=G4)
            m = dve.do(lambda e: e.tensor_tensor(dst, o[:, :, :, 0:HD], rsum[:, :, :].unsqueeze(3).to_broadcast([P, TB, G4, HD]), ALU.mult), [m, *held[f"ao{b % 2}"]])
            bank.free = (m,)
            held["rs"] = (m,)
            held["ao_in"] = m
            yield

        def finish(b):
            hs, s = h2[:, b % 3], b % 2
            bank, slot = (yield from misc.get()), turned_x.take()
            turned = transpose_tiles(lambda i: ao[:, s, i, :], bank, [held["ao_in"]])
            held[f"ao{s}"] = (turned,)
            m = act.do(lambda e: e.activation(slot.ap[:, :], bank.ap, ACT.Copy), [turned, *slot.free])
            bank.free = (m,)
            added = pool.do(lambda e: e.tensor_tensor(hs, hs, over_tiles(attn_row[:, :]), ALU.add), [ready[b][2], made_ready["attn_row"]])
            yield
            yield
            out_bank = yield from misc.get()
            p_o = per_tile_product(out_bank, lambda i: slot.ap[:, i * P:(i + 1) * P], Wqkv[:, W_O, :], [m])
            slot.free = (p_o,)
            yield
            m = dve.do(lambda e: e.tensor_tensor(flat(hs), flat(hs), out_bank.ap, ALU.add), [p_o, added])
            out_bank.free = (m,)
            yield
            dst = tiles(X1, b)
            normed = yield from normalise(hs, dst, stats_b[:, 1], mv_b[:, 1], rstd_b[:, 1], [m], ())
            h2_free[b % 3] = (normed,)
            m = pool.do(lambda e: e.tensor_tensor(dst, dst, over_tiles(row("g1")), ALU.mult), [normed])
            yield
            x1_in[b] = pool.do(lambda e: e.tensor_tensor(dst, dst, over_tiles(row("be1")), ALU.add), [m])
            yield
            yield
            yield

        def route(b):
            bank, slot = (yield from misc.get()), turned_x.take()
            turned = transpose_tiles(lambda i: X1[:, b * TB + i, :], bank, [x1_in[b]])
            x1T_in = act.do(lambda e: e.activation(slot.ap[:, :], bank.ap, ACT.Copy), [turned, *slot.free])
            bank.free = (x1T_in,)
            yield
            yield
            gate_bank = yield from misc.get()
            p_g = per_tile_product(gate_bank, lambda i: slot.ap[:, i * P:(i + 1) * P], Wg[:, :], [x1T_in], width=E)
            slot.free = (p_g,)
            yield
            wide = lambda ap: ap.unsqueeze(2).to_broadcast([P, TB, E])
            erow = lambda r: r.unsqueeze(1).to_broadcast([P, TB, E])
            pr, mask = t8[:, 0], t8[:, 1]
            top, total, inverse, best0, best1, rank = (t1[:, n] for n in range(6))
            hot_b = [hot[k][:, :, b * TB:(b + 1) * TB].rearrange("p e i -> p i e") for k in range(K)]
            v = chain(dve)
            m = v(lambda e: e.tensor_tensor(lg[:, :, :], gate_bank.ap[:, 0:TB * E].rearrange("p (i e) -> p i e", e=E), erow(bg_row[:, :]), ALU.add), [p_g, *held["small"]])
            gate_bank.free = (m,)
            v(lambda e: e.tensor_reduce(top, lg[:, :, :], AX.X, ALU.max))
            m = v(lambda e: e.tensor_tensor(lg[:, :, :], lg[:, :, :], wide(top), ALU.subtract))
            m = act.do(lambda e: e.activation(lg[:, :, :], lg[:, :, :], ACT.Exp), [m])
            yield
            yield
            v(lambda e: e.tensor_reduce(total, lg[:, :, :], AX.X, ALU.add), [m])
            v(lambda e: e.reciprocal(inverse, total))
            v(lambda e: e.tensor_tensor(pr, lg[:, :, :], wide(inverse), ALU.mult))
            yield
            for k, best in enumerate((best0, best1)):
                v(lambda e, best=best: e.tensor_reduce(best, pr, AX.X, ALU.max))
                v(lambda e, best=best: e.tensor_tensor(mask, pr, wide(best), ALU.is_equal))
                v(lambda e: e.tensor_tensor(mask, mask, erow(pri_row[:, :]), ALU.mult))
                yield
                v(lambda e: e.tensor_reduce(rank, mask, AX.X, ALU.max))
                m = v(lambda e, k=k: e.tensor_tensor(hot_b[k], mask, wide(rank), ALU.is_equal))
                if k == 0:
                    v(lambda e: e.scalar_tensor_tensor(out=pr, in0=hot_b[0], scalar=-2.0, in1=pr, op0=ALU.mult, op1=ALU.add))
                yield
            v(lambda e: e.tensor_tensor(total, best0, best1, ALU.add))
            v(lambda e: e.reciprocal(inverse, total))
            yield
            for k, best in enumerate((best0, best1)):
                m = v(lambda e, k=k, best=best: e.tensor_tensor(share[k][:, b * TB:(b + 1) * TB], best, inverse, ALU.mult))
            held["small"] = (m,)
            routed[b] = m
            yield

        scattered, tiles_known = {}, {}

        def sort_tokens(n, ring):
            b0, b1 = GROUPS[n]
            t0, nt, nj = b0 * TB, (b1 - b0) * TB, tiles_of[n]
            cnt, run = (t[:, 0:E * nt].rearrange("p (e i) -> p e i", e=E) for t in (counts, running))
            flat_c, flat_r = counts[:, 0:E * nt], running[:, 0:E * nt]
            n_of, tiles_e, ends, start, tmp = (e8[:, j] for j in range(5))
            v = chain(dve)
            v(lambda e: e.tensor_tensor(run, hot[0][:, :, t0:t0 + nt], hot[1][:, :, t0:t0 + nt], ALU.add), [routed[b1 - 1], *held["slots"]])
            bank_r, bank_c = (yield from ring.get()), (yield from ring.get())
            p_r = pe.do(lambda e: e.matmul(bank_r.ap[:, 0:E * nt], before[:, :], flat_r, start=True, stop=True), [(dve.sem, dve.count), *bank_r.free])
            p_c = pe.do(lambda e: e.matmul(bank_c.ap[:, 0:E * nt], ones[:, :], flat_r, start=True, stop=True), [*bank_c.free])
            yield
            yield
            m = v(lambda e: e.tensor_copy(flat_c, bank_c.ap[:, 0:E * nt]), [p_c, p_r])
            bank_c.free = (m,)
            yield
            v(lambda e: e.tensor_tensor_scan(flat_r, ones[:, 0:1].to_broadcast([P, E * nt]), flat_c, 0.0, ALU.mult, ALU.add))
            yield
            last = run[:, :, nt - 1]
            v(lambda e: e.tensor_copy(n_of[:, 0:1], last[:, 0:1]))
            v(lambda e: e.tensor_tensor(n_of[:, 1:E], last[:, 1:E], last[:, 0:E - 1], ALU.subtract))
            v(lambda e: e.tensor_scalar(tmp, n_of, float(P - 1), None, ALU.add))
            v(lambda e: e.tensor_copy(e8i[:, :], tmp))
            yield
            v(lambda e: e.tensor_scalar(e8i[:, :], e8i[:, :], P.bit_length() - 1, None, ALU.logical_shift_right))
            v(lambda e: e.tensor_copy(tiles_e, e8i[:, :]))
            v(lambda e: e.tensor_tensor_scan(ends, ones[:, 0:E], tiles_e, 0.0, ALU.mult, ALU.add))
            yield
            v(lambda e: e.tensor_tensor(tmp, ends, tiles_e, ALU.subtract))
            v(lambda e: e.scalar_tensor_tensor(out=start, in0=tmp, scalar=float(P), in1=last, op0=ALU.mult, op1=ALU.subtract))
            v(lambda e: e.tensor_tensor(start, start, n_of, ALU.add))
            yield
            v(lambda e: e.tensor_tensor(run, run, cnt, ALU.subtract))
            v(lambda e: e.tensor_tensor(run, run, start.unsqueeze(2).to_broadcast([P, E, nt]), ALU.add))
            yield
            m = v(lambda e: e.tensor_tensor(flat_r, flat_r, bank_r.ap[:, 0:E * nt], ALU.add))
            bank_r.free = (m,)
            yield
            for k in range(K):
                v(lambda e, k=k: e.tensor_tensor(cnt, run, hot[k][:, :, t0:t0 + nt], ALU.mult))
                yield
                v(lambda e: e.tensor_reduce(picks[:, 0:nt], cnt.rearrange("p e i -> p i e"), AX.X, ALU.add))
                placed = v(lambda e, k=k: e.tensor_copy(slot_of[k][:, t0:t0 + nt], picks[:, 0:nt]))
                yield
            cmp = compared[:, 0:nj, :]
            v(lambda e: e.tensor_tensor(cmp, tile_no[:, 0:nj].unsqueeze(2).to_broadcast([1, nj, E]), ends[0:1, :].unsqueeze(1).to_broadcast([1, nj, E]), ALU.is_ge), [weights_in])
            yield
            v(lambda e: e.tensor_reduce(tile_expert[:, 0:nj], cmp, AX.X, ALU.add))
            v(lambda e: e.tensor_scalar(tile_expert[:, 0:nj], tile_expert[:, 0:nj], float(E - 1), None, ALU.min))
            tiles_known[n] = v(lambda e: e.tensor_copy(expert_of[n][:, :], tile_expert[:, 0:nj]))
            held["slots"] = (tiles_known[n],)
            yield
            for t in range(t0, t0 + nt):
                for k in range(K):
                    pool.wait(placed, zeroed, x1_in[b1 - 1])
                    s_scatter[n].count += 16
                    pool.steps.append(lambda e, t=t, k=k: e.indirect_dma_start(
                        sorted_x[n], bass.IndirectOffsetOnAxis(ap=slot_of[k][:, t:t + 1], axis=0), X1[:, t, :], None).then_inc(s_scatter[n].sem, 16))
                    yield
            scattered[n] = (s_scatter[n].sem, s_scatter[n].count)

        units = [(b, g) for b in range(B) for g in range(G4)]
        run_beside([prepare(0)], 1)
        ahead = maxima()
        for _ in range(LEAD):
            next(ahead)
        later = []
        preparing = iter(())
        W1 = Region(nc, experts_at).place("W1_sb", [P, E, FF])
        W2 = Region(nc, experts_at + 4 * E * FF).place("W2_sb", [P, E, NF, D])
        b2_rows = Region(nc, b2_at).place("b2_rows", [P, E, D])
        assert B % 2 == 0

        def step_later():
            while later:
                if next(later[0], "ended") != "ended":
                    return
                later.pop(0)

        for n, (b, g) in enumerate(units):
            s = b % 2
            if g == 0:
                preparing = prepare(b + 1) if b + 1 < B else iter(())
            acc = pv_banks.take()

            def values(kt, slots):
                for G, (slot, mark) in enumerate(slots):
                    h = g * G4 + G
                    last = pe.do(lambda e, G=G, h=h, t=slot, s=s, acc=acc: e.matmul(
                        acc.ap[32 * G:32 * G + 32, :], vaug[s][:, kt, h, :], t.ap[:, :], start=kt == 0, stop=kt == TB - 1),
                        [mark, ready[b][1], *acc.free])
                    slot.free = (last,)
                return last

            waiting = None
            for kt in range(TB):
                slots = []
                for G in range(G4):
                    h = g * G4 + G
                    bank, slot = score_banks.take(), PT.take()
                    p_s = pe.do(lambda e, G=G, h=h, kt=kt, k=bank, s=s: e.matmul(k.ap, KS[s][:, G, kt * P:(kt + 1) * P], QS[s][:, h, :], start=True, stop=True),
                                [sent[n], *bank.free])
                    m = act.do(lambda e, k=bank, t=slot: e.activation(t.ap[:, :], k.ap, ACT.Exp, scale=SCORE_SCALE), [p_s, *slot.free])
                    bank.free = (m,)
                    slots.append((slot, m))
                    if waiting and G == PV_AT:
                        values(*waiting)
                    next(preparing, None)
                    next(ahead, None)
                    step_later()
                waiting = (kt, slots)
            last = values(*waiting)
            t_in = act.do(lambda e, k=acc: e.activation(oT[:, :], k.ap, ACT.Copy), [last, *held["oT"]])
            acc.free = (t_in,)
            later.insert(0, collect(b, g, t_in))
            step_later()
            if g == G4 - 1:
                v_read[s] = stack_read[s] = (last,)
                later += [finish(b), route(b)]
                if b == GROUPS[0][1] - 1:
                    later.append(sort_tokens(0, misc))
                if b == B - 2:
                    for e_ in range(E):
                        sp.dma(s_moe, W1[:, e_, :], a["W1"][e_], [last])
                        sp.dma(s_moe, W2[:, e_, :, :], a["W2"][e_].rearrange("(f p) d -> p f d", p=P))
                    moe_in = sp.dma(s_moe, b2_rows[:, :, :], a["b2"].partition_broadcast(P))

        units_done = [last, t_in]
        end = Region(nc, late_at)
        xs = Ring([Slot(end.place(f"xs{i}", [P, D])) for i in range(4)])
        xsT = Ring([Slot(end.place(f"xsT{i}", [P, P])) for i in range(2)])
        raw = Ring([Slot(end.place(f"raw{i}", [P, FF])) for i in range(2)])
        act_h = Ring([Slot(end.place(f"act_h{i}", [P, NF, P])) for i in range(2)])
        ys = Ring([Slot(end.place(f"ys{i}", [P, D])) for i in range(4)])
        back = [end.place(f"back{k}", [P, 2, TB, D]) for k in range(K)]
        fin = end.place("fin", [P, 2, TB, D])
        stats_c = end.place("stats_c", [P, 2, TB, 6])
        mv_c = end.place("mv_c", [P, 2, TB, 2])
        rstd_c = end.place("rstd_c", [P, 2, TB])
        assert end.at <= rest_at
        x_banks, h_banks, ht_banks = Ring(banks[0:1]), Ring(banks[1:3]), Ring(banks[3:5])
        y_banks = Ring([banks[5]])
        while later and scattered.get(0) is None:
            step_later()
        for bank in banks[0:6]:
            bank.free = (*bank.free, *units_done)
        for ring in (xs, xsT, raw, act_h, ys):
            for slot in ring.slots:
                slot.free = (*units_done,)
        later.append(sort_tokens(1, misc))
        stored = [{}, {}]

        def expert_tiles(n):
            nj = tiles_of[n]
            live = {}

            def load(j):
                slot = xs.take()
                live[j] = {"x": slot, "x_in": sp.dma(s_load[j % 4], slot.ap[:, :], sorted_x[n][j * P:(j + 1) * P, :], [scattered[n], *slot.free])}

            def turn(j):
                t, bank, slot = live[j], x_banks.take(), xsT.take()
                p = pe.do(lambda e: e.transpose(bank.ap[:, 0:P], t["x"].ap[:, :], ident[:, :]), [t["x_in"], *bank.free])
                t["x"].free = (p,)
                t["xT"], t["xT_in"] = slot, dve.do(lambda e: e.tensor_copy(slot.ap[:, :], bank.ap[:, 0:P]), [p, *slot.free])
                bank.free = (t["xT_in"],)

            def up(j):
                t, bank, slot = live[j], h_banks.take(), raw.take()
                pe.wait(t["xT_in"], moe_in, tiles_known[n], *bank.free)

                def product(e):
                    expert = e.value_load(expert_of[n][0:1, j:j + 1], min_val=0, max_val=E - 1)
                    t["pe_expert"] = expert
                    return e.matmul(bank.ap, t["xT"].ap[:, :], W1[:, bass.ds(expert, 1), :].rearrange("p o f -> p (o f)"), start=True, stop=True)
                p = pe.do(product)
                t["xT"].free = (p,)
                t["raw"], t["raw_in"] = slot, dve.do(lambda e: e.tensor_copy(slot.ap[:, :], bank.ap), [p, *slot.free])
                bank.free = (t["raw_in"],)

            def turn_hidden(j):
                t, bank, slot = live[j], ht_banks.take(), act_h.take()
                p = transpose_tiles(lambda f: t["raw"].ap[:, f * P:(f + 1) * P], bank, [t["raw_in"]])
                t["raw"].free = (p,)
                act.wait(p, tiles_known[n], *slot.free)
                for f in range(NF):
                    def gelu(e, f=f):
                        if f == 0:
                            t["act_expert"] = e.value_load(expert_of[n][0:1, j:j + 1], min_val=0, max_val=E - 1)
                        return e.activation(slot.ap[:, f, :], bank.ap[:, f * P:(f + 1) * P], ACT.Gelu,
                                            bias=b1c[:, bass.ds(t["act_expert"], 1), f:f + 1].rearrange("p o f -> p (o f)"))
                    m = act.do(gelu)
                bank.free = (m,)
                t["h"], t["h_in"] = slot, m

            def down(j):
                t, bank, slot = live.pop(j), y_banks.take(), ys.take()
                for f in range(NF):
                    p = pe.do(lambda e, f=f: e.matmul(bank.ap[:, 0:D], t["h"].ap[:, f, :], W2[:, bass.ds(t["pe_expert"], 1), f, :].rearrange("p o d -> p (o d)"),
                                                     start=f == 0, stop=f == NF - 1), [t["h_in"], *bank.free], signal=f == NF - 1)
                t["h"].free = (p,)

                def add_b2(e):
                    expert = e.value_load(expert_of[n][0:1, j:j + 1], min_val=0, max_val=E - 1)
                    return e.tensor_tensor(slot.ap[:, :], bank.ap[:, 0:D], b2_rows[:, bass.ds(expert, 1), :].rearrange("p o d -> p (o d)"), ALU.add)
                m = dve.do(add_b2, [p, moe_in, tiles_known[n], *slot.free])
                bank.free = (m,)
                out_mark = sp.dma(s_store[j % 4], sorted_y[n][j * P:(j + 1) * P, :], slot.ap[:, :], [m])
                slot.free = (out_mark,)
                stored[n][j % 4] = out_mark

            for j in range(nj + 4):
                if j < nj:
                    load(j)
                if 2 <= j < nj + 2:
                    up(j - 2)
                if 3 <= j < nj + 3:
                    turn_hidden(j - 3)
                if 4 <= j:
                    down(j - 4)
                if 1 <= j < nj + 1:
                    turn(j - 1)
                yield

        def combine(b, n):
            s = b % 2
            t0 = b * TB
            for k in range(K):
                for i in range(TB):
                    pool.wait(*stored[n].values(), *back_free[s])
                    s_gather[s].count += 16
                    pool.steps.append(lambda e, k=k, i=i: e.indirect_dma_start(
                        back[k][:, s, i, :], None, sorted_y[n], bass.IndirectOffsetOnAxis(ap=slot_of[k][:, t0 + i:t0 + i + 1], axis=0)).then_inc(s_gather[s].sem, 16))
                    yield
            fetched = (s_gather[s].sem, s_gather[s].count)
            xg = dve.do(lambda e: e.tensor_tensor(tiles(X, b), tiles(X, b), over_tiles(rows[:, b, GBE, :]), ALU.add), [made_ready["gg"]])
            yield
            yield
            for k in range(K):
                for i in range(TB):
                    m = dve.do(lambda e, k=k, i=i: e.scalar_tensor_tensor(
                        out=X1[:, t0 + i, :], in0=back[k][:, s, i, :], scalar=share[k][:, t0 + i:t0 + i + 1], in1=X1[:, t0 + i, :],
                        op0=ALU.mult, op1=ALU.add), [fetched, x1_in[b], (dve.sem, dve.count - TB + 1)] if k else [fetched, x1_in[b]])
                yield
            back_free[s] = (m,)
            normed = yield from normalise(tiles(X1, b), fin[:, s], stats_c[:, s], mv_c[:, s], rstd_c[:, s], [m], fin_free[s])
            m = dve.do(lambda e: e.tensor_tensor(fin[:, s], fin[:, s], over_tiles(rows[:, b, GG, :]), ALU.mult), [normed])
            yield
            m = dve.do(lambda e: e.tensor_tensor(fin[:, s], fin[:, s], tiles(X, b), ALU.add), [m, xg])
            fin_free[s] = (sp.dma(s_out[s], out_tiles[b], fin[:, s], [m]),)
            yield

        back_free, fin_free = [tuple(units_done), tuple(units_done)], [(), ()]
        for _ in expert_tiles(0):
            step_later()
            step_later()
            step_later()
        while later:
            step_later()
        assert 1 in scattered
        for bank in banks[6:8]:
            bank.free = (*bank.free,)
        for b in range(*GROUPS[0]):
            later.append(combine(b, 0))
        for _ in expert_tiles(1):
            for _ in range(4):
                step_later()
        while later:
            step_later()
        run_beside([combine(b, 1) for b in range(*GROUPS[1])], 2)
        sp.wait(*[(t.sem, t.count) for t in s_out])

        block = scope.enter_context(nc.Block())

        @block.sync
        def _(engine):
            sp.play(engine)

        @block.scalar
        def _(engine):
            act.play(engine)

        @block.vector
        def _(engine):
            dve.play(engine)

        @block.gpsimd
        def _(engine):
            pool.play(engine)

        @block.tensor
        def _(engine):
            pe.play(engine)


def _layout(inputs):
    import numpy as np

    g = {k: np.asarray(v) for k, v in inputs.items()}
    B, L, D = g["L0_attn_x"].shape
    E, _, FF = g["L0_ffn_W1"].shape
    H, HD = 16, D // 16
    order = np.array([(4 * gg + G) * HD + d for gg in range(4) for d in range(HD) for G in range(4)])
    swap = np.array([(c // HD) * HD + (c % HD + HD // 2) % HD for c in range(D)])
    rot = swap[order]
    d_of = order % HD
    inv = 1.0 / 10000.0 ** (np.arange(0, HD, 2, dtype=np.float32) / np.float32(HD))
    freqs = (np.arange(L, dtype=np.float32)[:, None] * inv.astype(np.float32)[None, :]).astype(np.float32)
    emb = np.concatenate([freqs, freqs], -1)
    cos, sin = np.cos(emb).astype(np.float32), np.sin(emb).astype(np.float32)
    sign = np.where(d_of < HD // 2, -1.0, 1.0).astype(np.float32)
    c = np.ascontiguousarray
    Wi = g["L0_attn_W_in"]
    return {
        "x": c(g["L0_attn_x"]), "cT": c(g["L0_c"].T), "wmod": c(g["L0_wmod"]),
        "ident": np.eye(D, dtype=np.float32), "priority": np.arange(E, 0, -1).astype(np.float32),
        "W_in_u": c(Wi[:D]), "W_gateT": c(Wi[D:].T), "W_stateT": c(g["L0_attn_W_state"].T), "W_dtT": c(g["L0_attn_W_dt"].T),
        "W_CT": c(g["L0_attn_W_C"].T), "W_outT": c(g["L0_attn_W_out"].T),
        "vecs": c(np.stack([g["L0_attn_b_dt"], g["L0_attn_A_log"], g["L0_attn_D"], g["L0_ffn_bq"][order], g["L0_ffn_bq"][rot],
                            g["L0_ffn_bk"][order], g["L0_ffn_bk"][rot], g["L0_ffn_bv"]], 1)),
        "before": np.triu(np.ones((128, 128), np.float32), 1), "tile_no": np.arange((2 * L * (B - 2) + E * 127) // 128, dtype=np.float32)[None],
        "Wq": c(g["L0_ffn_Wq"][:, order]), "Wq_rot": c(g["L0_ffn_Wq"][:, rot]),
        "Wk": c(g["L0_ffn_Wk"][:, order]), "Wk_rot": c(g["L0_ffn_Wk"][:, rot]),
        "Wv": c(g["L0_ffn_Wv"]), "Wo": c(g["L0_ffn_Wo"]), "bo": c(g["L0_ffn_bo"]),
        "cos": c(cos.T[d_of]), "sin": c(sin.T[d_of] * sign[:, None]),
        "g1": c(g["L0_ffn_g1"]), "be1": c(g["L0_ffn_be1"]), "g2": c(g["L0_ffn_g2"]), "be2": c(g["L0_ffn_be2"]),
        "Wg": c(g["L0_ffn_Wg"]), "bg": c(g["L0_ffn_bg"]), "W1": c(g["L0_ffn_W1"]), "W2": c(g["L0_ffn_W2"]),
        "b1T": c(g["L0_ffn_b1"].reshape(E, FF // 128, 128).transpose(2, 0, 1)), "b2": c(g["L0_ffn_b2"]),
    }


def kernel(**inputs):
    import concourse.bacc as _bacc
    from concourse import mybir as _mybir
    from concourse.bass_utils import run_bass_kernel_spmd as _run

    arrays = _layout(inputs)
    nc = _bacc.Bacc("TRN2", target_bir_lowering=False, num_devices=1)
    aps = {k: nc.dram_tensor(f"in_{k}", v.shape, _mybir.dt.from_np(v.dtype), kind="ExternalInput").ap() for k, v in arrays.items()}
    out = nc.dram_tensor("out_0", arrays["x"].shape, _mybir.dt.float32, kind="ExternalOutput").ap()
    adaln_block(nc, aps, out)
    r = _run(nc, [{f"in_{k}": v for k, v in arrays.items()}], core_ids=[0])
    return r.results[0]["out_0"]
```

```python
from contextlib import ExitStack

import concourse.bass as bass
from concourse import mybir

ALU = mybir.AluOpType
ACT = mybir.ActivationFunctionType
AX = mybir.AxisListType
F32 = mybir.dt.float32
F32R = mybir.dt.float32r
I32 = mybir.dt.int32

P = 128
LN_EPS = 1e-5
RATE_EPS = 1e-4
DT_MAX = 10.0
DT_CLAMP = 20.0
MIN_GATE = 0.25
BANK = 512
SMAX_BANKS = 3
MISC_BANKS = 2
REST = 1
PV_AT = 2
STACK_STEP = 2


class Queue:

    def __init__(self, sem):
        self.sem, self.count, self.steps, self.met = sem, 0, [], {}

    def wait(self, *marks):
        for sem, value in marks:
            if self.met.get(sem.name, 0) < value:
                self.met[sem.name] = value
                self.steps.append(lambda e, s=sem, v=value: e.wait_ge(s, v))

    def do(self, instruction, after=(), signal=True):
        self.wait(*after)
        if not signal:
            self.steps.append(instruction)
            return None
        self.count += 1
        self.steps.append(lambda e: instruction(e).then_inc(self.sem, 1))
        return (self.sem, self.count)

    def dma(self, stream, out, in_, after=()):
        self.wait(*after)
        stream.count += 16
        self.steps.append(lambda e: e.dma_start(out, in_).then_inc(stream.sem, 16))
        return (stream.sem, stream.count)

    def play(self, engine):
        for step in self.steps:
            step(engine)


class Stream:

    def __init__(self, sem):
        self.sem, self.count = sem, 0


class Slot:

    now = 0

    def __init__(self, ap):
        self.ap, self.marks, self.held, self.since = ap, (), False, 0

    @property
    def free(self):
        return self.marks

    @free.setter
    def free(self, marks):
        self.marks, self.held, self.since = tuple(marks), False, Slot.now


class Ring:

    def __init__(self, slots, rest=0):
        self.slots, self.n, self.rest = slots, 0, rest

    def may_take(self, slot):
        return not slot.held and Slot.now - slot.since >= self.rest

    def ready(self):
        return any(self.may_take(slot) for slot in self.slots)

    def take(self):
        assert self.ready(), "all slots taken"
        while not self.may_take(self.slots[self.n % len(self.slots)]):
            self.n += 1
        slot = self.slots[self.n % len(self.slots)]
        self.n += 1
        slot.held = True
        return slot

    def get(self):
        while not self.ready():
            yield
        return self.take()


class Region:

    def __init__(self, nc, start):
        self.nc, self.at = nc, start

    def place(self, name, shape, dtype=F32):
        size = 4
        for n in shape[1:]:
            size *= n
        start = (self.at + 31) // 32 * 32
        self.at = start + size
        assert self.at <= self.nc.sbuf_usable_end, (name, self.at)
        return self.nc.alloc_sbuf_tensor_at(name, shape, dtype, offset=start)


def pause(steps):
    for _ in range(steps):
        yield


def hastened(part, steps):
    while True:
        for _ in range(steps):
            if next(part, "ended") == "ended":
                return
        yield


def chained(parts):
    for part in parts:
        yield from part


def beside(parts, at_once):
    running, parts = [], list(parts)
    while parts or running:
        if parts and len(running) < at_once:
            running.append(parts.pop(0))
        for part in list(running):
            if next(part, "ended") == "ended":
                running.remove(part)
        yield


def run_beside(parts, at_once):
    for _ in beside(parts, at_once):
        pass

def adaln_block(nc, a, out):
    B, L, D = a["x"].shape
    TB = L // P
    NT = B * TB
    H = 16
    HD = D // H
    G4 = 4
    E, _, FF = a["W1"].shape
    NF = FF // P
    K = 2
    SCORE_SCALE = float(HD) ** -0.5
    DEEP = 4
    LEAD = 24
    BACKS = 4
    GATHER_TIME = 4
    AHEAD = 8
    NUMBERS = 8
    GROUPS = ((0, B - 2), (B - 2, B))
    assert D == P and L == BANK and H == G4 * G4 and 3 * HD < 32
    tiles_of = [(K * L * (hi - lo) + E * (P - 1)) // P for lo, hi in GROUPS]

    x_tiles = a["x"].rearrange("b (i p) d -> b p i d", p=P)
    out_tiles = out.rearrange("b (i p) d -> b p i d", p=P)
    sorted_x = [nc.dram_tensor(f"sorted_x{n}", [t * P, D], F32).ap() for n, t in enumerate(tiles_of)]
    sorted_y = [nc.dram_tensor(f"sorted_y{n}", [t * P, D], F32).ap() for n, t in enumerate(tiles_of)]

    with ExitStack() as scope:
        sem = lambda name: scope.enter_context(nc.semaphore(name))
        pe, act, dve, pool, sp = (Queue(sem(n)) for n in ("pe_done", "act_done", "dve_done", "pool_done", "sp_done"))
        stream = lambda name: Stream(sem(name))
        s_first, s_ssm, s_consts = stream("first_in"), stream("ssm_weights_in"), stream("consts_in")
        s_zero, s_moe = stream("zeroed"), stream("moe_weights_in")
        s_ones = [stream(f"ones_row_in_{n}") for n in range(2)]
        s_x = [stream(f"x_in_{b}") for b in range(B)]
        s_stack = [[stream(f"{part}_stack_in_{n}") for part in ("q", "k")] for n in range(2)]
        s_max = [stream(f"max_in_{n}") for n in range(4)]
        s_scatter = [stream(f"scattered_{n}") for n in range(2)]
        s_load = [stream(f"sorted_x_in_{n}") for n in range(AHEAD)]
        s_store = [[stream(f"sorted_y{n}_out_{i}") for i in range(4)] for n in range(2)]
        s_gather = [[stream(f"gathered_{n}_{k}") for k in range(K)] for n in range(BACKS)]
        s_out = [stream(f"out_stored_{n}") for n in range(2)]
        psum = scope.enter_context(nc.psum_tensor("psum", [P, 8, BANK], F32))
        banks = [Slot(psum[:, n, :]) for n in range(8)]

        keep = Region(nc, nc.sbuf_base)
        X = keep.place("X", [P, NT, D])
        ident = keep.place("ident", [P, P])
        rows = keep.place("rows", [P, B, 4, D])
        SB, CB, GG, GBE = range(4)
        vec_names = ["b_dt", "A_log", "Dskip", "bq", "bq_rot", "bk", "bk_rot", "bv"]
        vecs = keep.place("vecs_sb", [P, len(vec_names)])
        row_names = ["bo", "g1", "be1", "g2", "be2"]
        row_pack = keep.place("row_pack_sb", [P, len(row_names) * D + 2 * E])
        rowc = row_pack[:, 0:len(row_names) * D].rearrange("p (n d) -> p n d", d=D)
        bg_row = row_pack[:, len(row_names) * D:len(row_names) * D + E]
        pri_row = row_pack[:, len(row_names) * D + E:len(row_names) * D + 2 * E]
        W_Q, W_QR, W_K, W_KR, W_V, W_O = range(6)
        widths = [6 * D, L, L, P, E, E * NF]
        consts = keep.place("consts_sb", [P, sum(widths)])
        Wqkv, cos_t, sin_t, before, Wg, b1c = (consts[:, sum(widths[:n]):sum(widths[:n + 1])] for n in range(len(widths)))
        Wqkv = Wqkv.rearrange("p (n d) -> p n d", d=D)
        b1c = b1c.rearrange("p (e f) -> p e f", f=NF)
        modc = keep.place("modc", [P, 2, B])
        negrate = keep.place("negrate", [P, 1])
        half = keep.place("half", [P, TB])
        attn_row = keep.place("attn_row", [P, D])
        ones = keep.place("ones", [P, P])
        tile_no = keep.place("tile_no_sb", [1, max(tiles_of)])
        hot = [keep.place(f"hot{k}", [P, E, NT]) for k in range(K)]
        share = [keep.place(f"share{k}", [P, NT]) for k in range(K)]
        slot_of = [keep.place(f"slot_of{k}", [P, NT], I32) for k in range(K)]
        expert_of = [keep.place(f"expert_of{n}", [1, t], I32) for n, t in enumerate(tiles_of)]
        hT = Region(nc, keep.at).place("hT", [P, B, L])
        X1 = keep.place("X1", [P, NT, D])
        assert B * L == NT * D
        b2_at = keep.at
        QS, KS = [None, None], [None, None]
        KS[0] = keep.place("KS0", [P, G4, L], F32R)
        experts_at = keep.at
        QS[0] = keep.place("QS0", [P, H, L], F32R)
        late_at = keep.at
        KS[1] = keep.place("KS1", [P, G4, L], F32R)
        QS[1] = keep.place("QS1", [P, H, L], F32R)
        rest_at = keep.at

        ssm = Region(nc, rest_at)
        gate = ssm.place("gate", [P, B, L])
        Wssm = ssm.place("Wssm", [P, 6, D])
        W_INU, W_GATE, W_STATE, W_DT, W_C, W_OUT = range(6)
        Wfused = ssm.place("Wfused", [P, 2, D])
        Wout_b = ssm.place("Wout_b", [P, B, D])
        rate3 = ssm.place("rate3", [P, 3])
        setup = Region(nc, ssm.at)
        ssm_work = [{n: ssm.place(f"{n}_{i}", [P, L]) for n in ("dt", "ed")} for i in range(DEEP)]

        first_pack = setup.place("first_pack_sb", [P, B + 6 * D])
        cT, wmod = first_pack[:, 0:B], first_pack[:, B:B + 6 * D].rearrange("c (n d) -> c n d", n=6)
        silu_c = setup.place("silu_c", [P, B])
        silu_cb = setup.place("silu_cb", [P, B, P])
        bv_b = setup.place("bv_b", [P, P])
        gates = setup.place("gates", [P, 2, B, D])
        gsign = setup.place("gsign", [P, 2, B, D])
        stats_a = setup.place("stats_a", [P, DEEP, TB, 6])
        mv_a = setup.place("mv_a", [P, DEEP, TB, 2])
        rstd_a = setup.place("rstd_a", [P, DEEP, TB])
        xn_a = setup.place("xn_a", [P, DEEP, TB, D])

        early_at = ssm.at
        early = Region(nc, early_at)
        vaug0 = early.place("vaug0", [P, TB, H, 32])
        h2T_slot = Slot(early.place("h2T", [P, L]))
        rope = [early.place(f"rope{i}", [P, L]) for i in range(2)]
        hi_of = [early.place(f"hi{n}", [P, L], F32R) for n in range(2)]
        lo_of = [early.place(f"lo{n}", [P, L], F32R) for n in range(2)]
        stats_b = early.place("stats_b", [P, 2, TB, 6])
        mv_b = early.place("mv_b", [P, 2, TB, 2])
        rstd_b = early.place("rstd_b", [P, 2, TB])
        constrow = early.place("constrow", [G4 * TB, 2, P])

        col = lambda name: vecs[:, vec_names.index(name):vec_names.index(name) + 1]
        row = lambda name: rowc[:, row_names.index(name), :]
        over_tiles = lambda ap: ap.unsqueeze(1).to_broadcast([P, TB, D])
        tiles = lambda t, b: t[:, b * TB:(b + 1) * TB, :]
        flat = lambda ap: ap.rearrange("p i d -> p (i d)")

        sp.dma(s_first, first_pack[:, :], a["first_pack"])
        first_in = act.dma(s_first, ident[:, :], a["ident"])
        x_in = [sp.dma(s_x[0], tiles(X, 0), x_tiles[0])]
        sp.dma(s_ssm, Wssm[:, :, :], a["ssm_pack"].rearrange("c (n d) -> c n d", d=D))
        sp.dma(s_ssm, vecs[:, :], a["vecs"])
        ssm_in = sp.dma(s_ssm, row_pack[:, :], a["row_pack"].partition_broadcast(P))
        x_in += [sp.dma(s_x[b], tiles(X, b), x_tiles[b]) for b in range(1, B)]
        sp.dma(s_consts, consts[:, :], a["consts"])
        consts_in = sp.dma(s_consts, tile_no[:, :], a["tile_no"][:, 0:max(tiles_of)])

        half_set = dve.do(lambda e: e.memset(half[:, :], -0.5))
        ones_set = dve.do(lambda e: e.memset(ones[:, :], 1.0))
        cleared = [{}, {}]

        def clear_stacks(i):
            for t in (QS[i], KS[i]):
                for j in range(0, t.shape[1], 4):
                    cleared[i] = pool.do(lambda e, t=t, j=j: e.memset(t[:, j:j + 4, :].bitcast(F32), 0.0))
                    yield

        for _ in clear_stacks(0):
            pass
        for n, t in enumerate(tiles_of):
            zeroed = sp.dma(s_zero, sorted_x[n].rearrange("(p r) d -> p (r d)", p=P),
                            QS[0][:, :, :].bitcast(F32).rearrange("p h t -> p (h t)")[:, 0:t * D], [cleared[0]])

        def chain(queue):
            last = [()]

            def step(instruction, after=()):
                mark = queue.do(instruction, [*last[0], *after])
                last[0] = (mark,)
                return mark
            return step

        def normalise(src, dst, stats, mv, rstd, after, free):
            for i in range(TB):
                seen = dve.do(lambda e, i=i: e.bn_stats(stats[:, i, :], src[:, i, :]), [*after, *free])
            yield
            for i in range(TB):
                summed = dve.do(lambda e, i=i: e.bn_aggr(mv[:, i, :], stats[:, i, :]), [seen])
            with_eps = pool.do(lambda e: e.tensor_scalar(rstd[:, :], mv[:, :, 1], LN_EPS, None, ALU.add), [summed])
            powered = pool.do(lambda e: e.tensor_tensor(rstd[:, :], rstd[:, :], half[:, :], ALU.pow), [with_eps, half_set])
            yield
            yield
            yield
            for i in range(TB):
                done = dve.do(lambda e, i=i: e.tensor_scalar(
                    dst[:, i, :], src[:, i, :], mv[:, i, 0:1], rstd[:, i:i + 1], ALU.subtract, ALU.mult), [powered])
            return done

        def transpose_tiles(src, bank, after):
            for i in range(TB):
                done = pe.do(lambda e, i=i: e.transpose(bank.ap[:, i * P:(i + 1) * P], src(i), ident[:, :]),
                             [*after, *bank.free], signal=i == TB - 1)
            return done

        def per_tile_product(bank, lhsT, rhs, after, width=D):
            for i in range(TB):
                done = pe.do(lambda e, i=i: e.matmul(bank.ap[:, i * width:(i + 1) * width], lhsT(i), rhs, start=True, stop=True),
                             [*after, *bank.free], signal=i == TB - 1)
            return done

        silued = act.do(lambda e: e.activation(silu_c[:, :], cT[:, :], ACT.Silu), [first_in])
        for n in range(2):
            mods = pe.do(lambda e, n=n: e.matmul(banks[0].ap[:, n * B:(n + 1) * B], wmod[:, n, :], silu_c[:, :], start=True, stop=True), [silued])
        mod_sa = dve.do(lambda e: e.tensor_copy(modc[:, 0, :], banks[0].ap[:, 0:B]), [mods])
        mod_ready = dve.do(lambda e: e.tensor_scalar(modc[:, 1, :], banks[0].ap[:, B:2 * B], 1.0, None, ALU.add), [mods])
        banks[0].free = (mod_sa, mod_ready)
        made_ready = {}

        def make_rows():
            for b in range(B):
                spread = dve.do(lambda e, b=b: e.tensor_scalar(silu_cb[:, b, :], ones[:, :], silu_c[:, b:b + 1], None, ALU.mult), [silued, ones_set])
            yield
            for b in range(B):
                bank = banks[6 + b % 2]
                made = pe.do(lambda e, b=b, k=bank: e.matmul(k.ap, silu_cb[:, b, :], wmod[:, 2:6, :].rearrange("c n d -> c (n d)"),
                                                            start=True, stop=True), [spread, *bank.free])
                sb_cb = act.do(lambda e, b=b, k=bank: e.activation(rows[:, b, SB:CB + 1, :], k.ap[:, D:3 * D].rearrange("p (n d) -> p n d", n=2), ACT.Copy), [made])
                ga_in = act.do(lambda e, b=b, k=bank: e.activation(gates[:, 0, b, :], k.ap[:, 0:D], ACT.Copy), [made])
                gb_in = act.do(lambda e, b=b, k=bank: e.activation(gates[:, 1, b, :], k.ap[:, 3 * D:4 * D], ACT.Copy), [made])
                bank.free = (gb_in, ga_in, sb_cb)
                yield
            g, sgn = gates[:, :, :, :].rearrange("p n b d -> p (n b d)"), gsign[:, :, :, :].rearrange("p n b d -> p (n b d)")
            signed = dve.do(lambda e: e.tensor_scalar(sgn, g, 0.0, 2.0, ALU.is_ge, ALU.mult), [ga_in, gb_in])
            yield
            m = dve.do(lambda e: e.scalar_tensor_tensor(out=g, in0=g, scalar=-1.0, in1=g, op0=ALU.mult, op1=ALU.max), [signed])
            yield
            m = dve.do(lambda e: e.tensor_scalar(g, g, MIN_GATE, None, ALU.max), [m])
            yield
            m = dve.do(lambda e: e.scalar_tensor_tensor(out=g, in0=sgn, scalar=-1.0, in1=g, op0=ALU.add, op1=ALU.mult), [m])
            gates_ready = m
            yield
            made_ready["cb"] = pool.do(lambda e: e.tensor_scalar(rows[:, :, CB, :], rows[:, :, CB, :], 1.0, 1.0, ALU.add, ALU.mult), [sb_cb])
            over_rows = lambda ap: ap.unsqueeze(1).to_broadcast([P, B, D])
            made_ready["Wout"] = dve.do(lambda e: e.tensor_tensor(Wout_b[:, :, :], gates[:, 0, :, :], over_rows(Wssm[:, W_OUT, :]), ALU.mult), [gates_ready, ssm_in])
            yield
            gg = pool.do(lambda e: e.tensor_tensor(rows[:, :, GG, :], gates[:, 1, :, :], over_rows(row("g2")), ALU.mult), [gates_ready, ssm_in, gb_in])
            made_ready["gg"] = pool.do(lambda e: e.tensor_tensor(rows[:, :, GBE, :], gates[:, 1, :, :], over_rows(row("be2")), ALU.mult), [gg])
            fused_bank = banks[6]
            for n, wi in enumerate((W_STATE, W_DT)):
                fused = pe.do(lambda e, n=n, wi=wi: e.matmul(fused_bank.ap[:, n * D:(n + 1) * D], Wssm[:, W_INU, :], Wssm[:, wi, :], start=True, stop=True), [ssm_in, *fused_bank.free])
            made_ready["fused"] = dve.do(lambda e: e.tensor_copy(Wfused[:, :, :].rearrange("p n d -> p (n d)"), fused_bank.ap[:, 0:2 * D]), [fused])
            fused_bank.free = (made_ready["fused"],)
            m = dve.do(lambda e: e.scalar_tensor_tensor(out=rate3[:, 0:1], in0=col("A_log"), scalar=-1.0, in1=col("A_log"), op0=ALU.mult, op1=ALU.min), [ssm_in])
            made_ready["A"] = dve.do(lambda e: e.tensor_scalar(rate3[:, 1:2], col("A_log"), 0.0, None, ALU.max), [m])
            bv_spread = dve.do(lambda e: e.tensor_scalar(bv_b[:, :], ones[:, :], col("bv"), None, ALU.mult), [ssm_in, ones_set])
            row_bank = banks[7]
            bv_wo = pe.do(lambda e: e.matmul(row_bank.ap[:, 0:D], bv_b[:, :], Wqkv[:, W_O, :], start=True, stop=True), [bv_spread, consts_in, *row_bank.free])
            made_ready["attn_row"] = dve.do(lambda e: e.tensor_tensor(attn_row[:, :], row_bank.ap[:, 0:D], row("bo"), ALU.add), [bv_wo])
            row_bank.free = (made_ready["attn_row"],)
            yield

        hT_in, gated, x2_in = {}, {}, {}
        a_free = [() for _ in range(DEEP)]
        turn_banks, gate_banks = Ring(banks[0:3]), Ring(banks[3:6])

        def first_part(b):
            s = b % DEEP
            xn = xn_a[:, s]
            normed = yield from normalise(tiles(X, b), xn, stats_a[:, s], mv_a[:, s], rstd_a[:, s], [x_in[b]], a_free[s])
            yield
            bank = turn_banks.take()
            turned = transpose_tiles(lambda i: xn[:, i, :], bank, [normed, first_in])
            a_free[s] = (turned,)
            yield
            hT_in[b] = act.do(lambda e: e.activation(hT[:, b, :], bank.ap, ACT.Identity, bias=modc[:, 0, b:b + 1], scale=modc[:, 1, b:b + 1]),
                              [turned, mod_sa, mod_ready])
            bank.free = (hT_in[b],)
            yield
            out_bank = gate_banks.take()
            product = pe.do(lambda e: e.matmul(out_bank.ap, Wssm[:, W_GATE, :], hT[:, b, :], start=True, stop=True), [hT_in[b], ssm_in, *out_bank.free])
            yield
            gated[b] = act.do(lambda e: e.activation(gate[:, b, :], out_bank.ap, ACT.Silu), [product])
            out_bank.free = (gated[b],)

        run_beside([make_rows()] + [first_part(b) for b in range(B)], DEEP + 1)
        first_done = [(q.sem, q.count) for q in (pe, act, dve, pool)]

        act.steps.append(lambda e: e.preload_act_table_set("natural_log_exp_and_others"))
        m = act.do(lambda e: e.activation(rate3[:, 2:3], rate3[:, 0:1], ACT.Exp), [made_ready["A"]])
        m = act.do(lambda e: e.activation(rate3[:, 2:3], rate3[:, 2:3], ACT.Ln, bias=1.0), [m])
        m = dve.do(lambda e: e.tensor_tensor(rate3[:, 2:3], rate3[:, 2:3], rate3[:, 1:2], ALU.add), [m])
        rate_ready = dve.do(lambda e: e.tensor_scalar(negrate[:, :], rate3[:, 2:3], RATE_EPS, -1.0, ALU.add, ALU.mult), [m])
        ssm_free = [{n: (*first_done,) for n in w} for w in ssm_work]
        for bank in banks:
            bank.free = (*first_done,)
        dt_banks, b_banks = Ring(banks[0:2]), Ring(banks[2:4])
        y_banks, o_banks, misc = Ring(banks[4:5]), Ring(banks[5:6]), Ring(banks[6:8])
        ssm_ends = []

        def second_part(b):
            s = b % DEEP
            dt, ed, z = ssm_work[s]["dt"], ssm_work[s]["ed"], gate[:, b, :]
            free = ssm_free[s]
            bank_dt = dt_banks.take()
            p_dt = pe.do(lambda e: e.matmul(bank_dt.ap, Wfused[:, 1, :], hT[:, b, :], start=True, stop=True), [hT_in[b], made_ready["fused"], *bank_dt.free])
            yield
            m = dve.do(lambda e: e.tensor_scalar(dt[:, :], bank_dt.ap, col("b_dt"), DT_CLAMP, ALU.add, ALU.min), [p_dt, *free["dt"]])
            bank_dt.free = (m,)
            yield
            m = act.do(lambda e: e.activation(ed[:, :], dt[:, :], ACT.Exp), [m, *free["ed"]])
            m = act.do(lambda e: e.activation(dt[:, :], ed[:, :], ACT.Ln, bias=1.0), [m])
            yield
            m = pool.do(lambda e: e.tensor_scalar(ed[:, :], dt[:, :], DT_MAX, negrate[:, 0:1], ALU.min, ALU.mult), [m, rate_ready])
            yield
            m = act.do(lambda e: e.activation(ed[:, :], ed[:, :], ACT.Exp), [m])
            bank_b = b_banks.take()
            p_b = pe.do(lambda e: e.matmul(bank_b.ap, Wfused[:, 0, :], hT[:, b, :], start=True, stop=True), [*bank_b.free])
            yield
            m = dve.do(lambda e: e.tensor_scalar(ed[:, :], ed[:, :], 0.0, 1.0, ALU.max, ALU.min), [m])
            m = dve.do(lambda e: e.scalar_tensor_tensor(out=dt[:, :], in0=ed[:, :], scalar=-1.0, in1=bank_b.ap, op0=ALU.add, op1=ALU.mult), [m, p_b])
            bank_b.free = (m,)
            yield
            m = dve.do(lambda e: e.tensor_tensor_scan(dt[:, :], ed[:, :], dt[:, :], 0.0, ALU.mult, ALU.subtract), [m])
            free["ed"] = (m,)
            yield
            bank_y = y_banks.take()
            p_y = pe.do(lambda e: e.matmul(bank_y.ap, Wssm[:, W_C, :], dt[:, :], start=True, stop=True), [m, *bank_y.free])
            free["dt"] = (p_y,)
            yield
            m = dve.do(lambda e: e.tensor_tensor(z, bank_y.ap, z, ALU.mult), [p_y, gated[b]])
            bank_y.free = (m,)
            yield
            m = dve.do(lambda e: e.scalar_tensor_tensor(out=z, in0=hT[:, b, :], scalar=col("Dskip"), in1=z, op0=ALU.mult, op1=ALU.add), [m])
            yield
            bank_o = o_banks.take()
            p_o = per_tile_product(bank_o, lambda i: z[:, i * P:(i + 1) * P], Wout_b[:, b, :], [m, made_ready["Wout"]])
            yield
            x2_in[b] = dve.do(lambda e: e.tensor_tensor(flat(tiles(X, b)), flat(tiles(X, b)), bank_o.ap, ALU.add), [p_o])
            bank_o.free = (x2_in[b],)
            ssm_ends[:] = [x2_in[b], p_o]

        HI1, HI2, LO, MAXROW = 0, HD, 2 * HD, 3 * HD
        VW = 32
        ones_row, zero_row = constrow[:, 1, :], constrow[:, 0, :]
        row_set = [dve.do(lambda e: e.memset(zero_row, 0.0), first_done), dve.do(lambda e: e.memset(ones_row, 1.0), first_done)]

        def set_ones(i):
            for g in range(G4):
                r = 32 * g + MAXROW
                ones_in[i] = sp.dma(s_ones[i], KS[i][r:r + 1, :, :].bitcast(F32), ones_row, [*row_set, cleared[i], zeroed])

        ones_in = [None, None]
        set_ones(0)
        v_ones = pool.do(lambda e: e.memset(vaug0[:, :, :, HD:VW], 0.0), first_done)
        v_ones = pool.do(lambda e: e.memset(vaug0[:, :, :, HD:HD + 1], 1.0), [v_ones])
        v_set = [(v_ones,), None]

        stack_read = [(), ()]
        v_read = [(), ()]
        held = {k: () for k in ("parts0", "parts1", "max0", "max1", "oT", "ao0", "ao1", "rs", "rope0", "rope1", "small", "slots")}
        ready, sent, x1_in, routed = {}, {}, {}, {}
        collected = [0] * B
        left = set()

        def prepare(b):
            s, hs = b % 2, tiles(X1, b)
            vaug_b = vaug[s] if b else vaug0
            while b not in x2_in:
                yield
            normed = yield from normalise(tiles(X, b), hs, stats_b[:, 0], mv_b[:, 0], rstd_b[:, 0], [x2_in[b], *(ssm_done if b else first_done)], ())
            m = pool.do(lambda e: e.tensor_tensor(hs, hs, over_tiles(rows[:, b, CB, :]), ALU.mult), [normed, made_ready["cb"]])
            yield
            h2_in = pool.do(lambda e: e.tensor_tensor(hs, hs, over_tiles(rows[:, b, SB, :]), ALU.add), [m])
            yield from pause(5)
            bank, slot = (yield from misc.get()), h2T_slot
            turned = transpose_tiles(lambda i: hs[:, i, :], bank, [h2_in])
            h2T = slot.ap
            h2T_in = act.do(lambda e: e.activation(h2T[:, :], bank.ap, ACT.Copy), [turned, *slot.free])
            bank.free = (h2T_in,)
            yield
            yield
            for n, (wp, wr, bp, br) in enumerate(((W_Q, W_QR, "bq", "bq_rot"), (W_K, W_KR, "bk", "bk_rot"))):
                hi, lo = hi_of[n], lo_of[n]

                def rope_half(j, w_, bias, table):
                    bank = yield from misc.get()
                    p = pe.do(lambda e: e.matmul(bank.ap, Wqkv[:, w_, :], h2T[:, :], start=True, stop=True), [h2T_in, *bank.free])
                    m = dve.do(lambda e: e.scalar_tensor_tensor(out=rope[j][:, :], in0=bank.ap, scalar=col(bias), in1=table[:, :],
                                                                op0=ALU.add, op1=ALU.mult), [p, *held[f"rope{j}"]])
                    bank.free = (m,)
                    return m
                m1 = yield from rope_half(0, wp, bp, cos_t)
                yield
                yield
                m2 = yield from rope_half(1, wr, br, sin_t)
                yield
                yield
                m3 = pool.do(lambda e: e.tensor_tensor(rope[0][:, :], rope[0][:, :], rope[1][:, :], ALU.add), [m1, m2])
                held["rope1"] = (m3,)
                yield
                yield
                m4 = dve.do(lambda e, hi=hi: e.tensor_copy(hi[:, :], rope[0][:, :]), [m3, *held[f"parts{n}"]])
                yield
                m5 = pool.do(lambda e, hi=hi, lo=lo: e.tensor_tensor(lo[:, :], rope[0][:, :], hi[:, :].bitcast(F32), ALU.subtract), [m4, *held[f"parts{n}"]])
                held["rope0"] = (m5,)
                yield
                while b - 2 not in left and b >= 2:
                    yield
                rows_of = ((HI1, hi), (HI2, hi), (LO, lo)) if n == 0 else ((HI1, hi), (LO, hi), (HI2, lo))
                if n == 0 and b >= 2:
                    for g in range(G4):
                        r = 32 * g + MAXROW
                        sp.dma(s_stack[s][n], QS[s][r:r + 1, g * G4:(g + 1) * G4, :].bitcast(F32), zero_row, [*row_set, cleared[s], zeroed, *stack_read[s]])
                        if g % 2:
                            yield
                for g in range(G4):
                    for r, part in rows_of:
                        r0 = 32 * g + r
                        dst = QS[s][r0:r0 + HD, g * G4:(g + 1) * G4, :] if n == 0 else KS[s][r0:r0 + HD, :, :]
                        stacked = sp.dma(s_stack[s][n], dst.bitcast(F32), part[32 * g:32 * g + 32, :].bitcast(F32),
                                        [m4 if part is hi else m5, cleared[s], zeroed, *stack_read[s]])
                        if r == LO:
                            yield
                    if g % 2:
                        yield
                held[f"parts{n}"] = (stacked,)
                yield
            q_stacked, = held["parts0"]
            v_bank = yield from misc.get()
            p_v = per_tile_product(v_bank, lambda i: h2T[:, i * P:(i + 1) * P], Wqkv[:, W_V, :], [h2T_in])
            slot.free = (p_v,)
            yield
            v_in = act.do(lambda e: e.activation(vaug_b[:, :, :, 0:HD], v_bank.ap.rearrange("p (i h d) -> p i h d", i=TB, h=H), ACT.Copy), [p_v, *v_set[s], *v_read[s]])
            v_bank.free = (v_in,)
            ready[b] = (stacked, v_in, h2_in, q_stacked)
            yield

        run_beside([*(second_part(b) for b in range(DEEP)), hastened(prepare(0), 3), clear_stacks(1), *(second_part(b) for b in range(DEEP, B))], DEEP + 2)
        set_ones(1)
        ssm_done = [*ssm_ends, (pool.sem, pool.count), (act.sem, act.count), (dve.sem, dve.count)]
        for bank in banks:
            bank.free = (*bank.free, *ssm_done)

        mid = Region(nc, rest_at)
        vaug = [vaug0, mid.place("vaug1", [P, TB, H, VW])]
        PT = Ring([Slot(mid.place(f"PT{i}", [P, L])) for i in range(8)])
        turned_x = Ring([Slot(mid.place("turned_x", [P, L]))])
        negmax = mid.place("negmax", [P, 2, G4 * TB])
        maxT = mid.place("maxT", [G4 * TB, 2, P], F32R)
        oT = mid.place("oT", [P, L])
        rsum = mid.place("rsum", [P, TB, G4])
        ao = mid.place("ao", [P, 2, TB, D])
        lg = mid.place("lg", [P, TB, E])
        t8 = mid.place("t8", [P, 2, TB, E])
        t1 = mid.place("t1", [P, 6, TB])
        NTG = max(h - l for l, h in GROUPS) * TB
        sorting = mid
        counts = sorting.place("counts", [P, E * NTG])
        running = sorting.place("running", [P, E * NTG])
        ranks = sorting.place("ranks", [P, E * NTG])
        e8 = sorting.place("e8", [P, 5, E])
        e8i = sorting.place("e8i", [P, E], I32)
        picks = sorting.place("picks", [P, NTG])
        compared = sorting.place("compared", [1, max(tiles_of), E])
        tile_expert = sorting.place("tile_expert", [1, max(tiles_of)])

        assert mid.at <= early_at
        misc = Ring(banks[8 - MISC_BANKS:8], REST)
        smax_banks, score_banks, pv_banks = Ring(banks[0:SMAX_BANKS]), Ring(banks[SMAX_BANKS:7 - MISC_BANKS]), Ring(banks[7 - MISC_BANKS:8 - MISC_BANKS])
        v_ones = pool.do(lambda e: e.memset(vaug[1][:, :, :, HD:VW], 0.0), ssm_done)
        v_ones = pool.do(lambda e: e.memset(vaug[1][:, :, :, HD:HD + 1], 1.0), [v_ones])
        v_set[1] = (v_ones,)

        def maxima():
            pending = []
            for n, (b, g) in enumerate(units):
                s, t = b % 2, n % 2
                while b not in ready:
                    yield
                for G in range(G4):
                    h = g * G4 + G
                    for i in range(TB):
                        bank = smax_banks.take()
                        p_s = pe.do(lambda e, G=G, h=h, i=i, k=bank, s=s: e.matmul(k.ap, QS[s][:, h, i * P:(i + 1) * P], KS[s][:, G, :], start=True, stop=True),
                                    [ready[b][0], ready[b][3], ones_in[s], *bank.free])
                        found = dve.do(lambda e, c=G * TB + i, k=bank, t=t: e.tensor_reduce(negmax[:, t, c:c + 1], k.ap, AX.X, ALU.max, negate=True), [p_s, *held[f"max{t}"]])
                        bank.free = (found,)
                        if pending and G * TB + i >= 3 and (pending[0][0] or misc.ready()):
                            pending.pop(0)[1]()
                        yield
                state = {}

                def turn(t=t, found=found, state=state):
                    bank = state["bank"] = misc.take()
                    state["turned"] = pe.do(lambda e: e.transpose(bank.ap[0:G4 * TB, 0:P], negmax[:, t, :], ident[:, :]), [found, *bank.free])
                    m = dve.do(lambda e: e.tensor_copy(maxT[:, t, :], bank.ap[0:G4 * TB, 0:P]), [state["turned"], *held[f"max{t}"]])
                    bank.free = (m,)
                    state["m"] = m

                def send(n=n, b=b, g=g, s=s, t=t, state=state, last=p_s):
                    r = 32 * g + MAXROW
                    sent[n] = sp.dma(s_max[n % 4], QS[s][r:r + 1, g * G4:(g + 1) * G4, :].bitcast(F32), maxT[:, t, :].bitcast(F32), [state["m"], last])
                    held[f"max{t}"] = (sent[n],)
                pending = [(False, turn), (True, send)]
            while pending:
                if pending[0][0] or misc.ready():
                    pending.pop(0)[1]()
                yield

        def collect(b, g, t_in):
            yield
            yield
            bank = yield from misc.get()
            turned = transpose_tiles(lambda i: oT[:, i * P:(i + 1) * P], bank, [t_in])
            held["oT"] = (turned,)
            o = bank.ap.rearrange("p (i j r) -> p i j r", i=TB, j=G4)
            yield
            m = dve.do(lambda e: e.reciprocal(rsum[:, :, :].unsqueeze(3), o[:, :, :, HD:HD + 1]), [turned, *held["rs"]])
            yield
            dst = ao[:, b % 2, :, 32 * g:32 * g + 32].rearrange("p i (j d) -> p i j d", j=G4)
            m = dve.do(lambda e: e.tensor_tensor(dst, o[:, :, :, 0:HD], rsum[:, :, :].unsqueeze(3).to_broadcast([P, TB, G4, HD]), ALU.mult), [m, *held[f"ao{b % 2}"]])
            bank.free = (m,)
            held["rs"] = (m,)
            held["ao_in"] = m
            collected[b] += 1

        def finish(b):
            hs, s = tiles(X1, b), b % 2
            bank, slot = (yield from misc.get()), turned_x.take()
            turned = transpose_tiles(lambda i: ao[:, s, i, :], bank, [held["ao_in"]])
            held[f"ao{s}"] = (turned,)
            m = act.do(lambda e: e.activation(slot.ap[:, :], bank.ap, ACT.Copy), [turned, *slot.free])
            bank.free = (m,)
            added = pool.do(lambda e: e.tensor_tensor(hs, hs, over_tiles(attn_row[:, :]), ALU.add), [ready[b][2], made_ready["attn_row"]])
            yield
            yield
            out_bank = yield from misc.get()
            p_o = per_tile_product(out_bank, lambda i: slot.ap[:, i * P:(i + 1) * P], Wqkv[:, W_O, :], [m])
            slot.free = (p_o,)
            yield
            m = dve.do(lambda e: e.tensor_tensor(flat(hs), flat(hs), out_bank.ap, ALU.add), [p_o, added])
            out_bank.free = (m,)
            yield
            dst = tiles(X1, b)
            normed = yield from normalise(hs, dst, stats_b[:, 1], mv_b[:, 1], rstd_b[:, 1], [m], ())
            m = pool.do(lambda e: e.tensor_tensor(dst, dst, over_tiles(row("g1")), ALU.mult), [normed])
            yield
            x1_in[b] = pool.do(lambda e: e.tensor_tensor(dst, dst, over_tiles(row("be1")), ALU.add), [m])
            yield from pause(6)

        def route(b):
            bank, slot = (yield from misc.get()), turned_x.take()
            turned = transpose_tiles(lambda i: X1[:, b * TB + i, :], bank, [x1_in[b]])
            x1T_in = act.do(lambda e: e.activation(slot.ap[:, :], bank.ap, ACT.Copy), [turned, *slot.free])
            bank.free = (x1T_in,)
            yield
            yield
            gate_bank = yield from misc.get()
            p_g = per_tile_product(gate_bank, lambda i: slot.ap[:, i * P:(i + 1) * P], Wg[:, :], [x1T_in], width=E)
            slot.free = (p_g,)
            yield
            wide = lambda ap: ap.unsqueeze(2).to_broadcast([P, TB, E])
            erow = lambda r: r.unsqueeze(1).to_broadcast([P, TB, E])
            pr, mask = t8[:, 0], t8[:, 1]
            top, total, inverse, best0, best1, rank = (t1[:, n] for n in range(6))
            hot_b = [hot[k][:, :, b * TB:(b + 1) * TB].rearrange("p e i -> p i e") for k in range(K)]
            v = chain(dve)
            m = v(lambda e: e.tensor_tensor(lg[:, :, :], gate_bank.ap[:, 0:TB * E].rearrange("p (i e) -> p i e", e=E), erow(bg_row[:, :]), ALU.add), [p_g, *held["small"]])
            yield
            gate_bank.free = (m,)
            v(lambda e: e.tensor_reduce(top, lg[:, :, :], AX.X, ALU.max))
            yield
            m = v(lambda e: e.tensor_tensor(lg[:, :, :], lg[:, :, :], wide(top), ALU.subtract))
            yield
            m = act.do(lambda e: e.activation(lg[:, :, :], lg[:, :, :], ACT.Exp), [m])
            yield
            yield
            v(lambda e: e.tensor_reduce(total, lg[:, :, :], AX.X, ALU.add), [m])
            yield
            v(lambda e: e.reciprocal(inverse, total))
            yield
            v(lambda e: e.tensor_tensor(pr, lg[:, :, :], wide(inverse), ALU.mult))
            yield
            for k, best in enumerate((best0, best1)):
                v(lambda e, best=best: e.tensor_reduce(best, pr, AX.X, ALU.max))
                yield
                v(lambda e, best=best: e.tensor_tensor(mask, pr, wide(best), ALU.is_equal))
                yield
                v(lambda e: e.tensor_tensor(mask, mask, erow(pri_row[:, :]), ALU.mult))
                yield
                v(lambda e: e.tensor_reduce(rank, mask, AX.X, ALU.max))
                yield
                m = v(lambda e, k=k: e.tensor_tensor(hot_b[k], mask, wide(rank), ALU.is_equal))
                yield
                if k == 0:
                    v(lambda e: e.scalar_tensor_tensor(out=pr, in0=hot_b[0], scalar=-2.0, in1=pr, op0=ALU.mult, op1=ALU.add))
                yield
            v(lambda e: e.tensor_tensor(total, best0, best1, ALU.add))
            yield
            v(lambda e: e.reciprocal(inverse, total))
            yield
            for k, best in enumerate((best0, best1)):
                m = v(lambda e, k=k, best=best: e.tensor_tensor(share[k][:, b * TB:(b + 1) * TB], best, inverse, ALU.mult))
                yield
            held["small"] = (m,)
            routed[b] = m
            yield

        scattered, tiles_known = {}, {}

        def sort_tokens(n, ring):
            b0, b1 = GROUPS[n]
            t0, nt, nj = b0 * TB, (b1 - b0) * TB, tiles_of[n]
            cnt, run = (t[:, 0:E * nt].rearrange("p (e i) -> p e i", e=E) for t in (counts, running))
            flat_c, flat_r = counts[:, 0:E * nt], running[:, 0:E * nt]
            n_of, tiles_e, ends, start, tmp = (e8[:, j] for j in range(5))
            v = chain(dve)
            v(lambda e: e.tensor_tensor(run, hot[0][:, :, t0:t0 + nt], hot[1][:, :, t0:t0 + nt], ALU.add), [routed[b1 - 1], *held["slots"]])
            bank = yield from ring.get()
            p_r = pe.do(lambda e: e.matmul(bank.ap[:, 0:E * nt], before[:, :], flat_r, start=True, stop=True), [(dve.sem, dve.count), *bank.free])
            p_c = pe.do(lambda e: e.matmul(bank.ap[:, E * nt:2 * E * nt], ones[:, :], flat_r, start=True, stop=True))
            yield
            yield
            v(lambda e: e.tensor_copy(flat_c, bank.ap[:, E * nt:2 * E * nt]), [p_c, p_r])
            bank.free = (v(lambda e: e.tensor_copy(ranks[:, 0:E * nt], bank.ap[:, 0:E * nt])),)
            yield
            v(lambda e: e.tensor_tensor_scan(flat_r, ones[:, 0:1].to_broadcast([P, E * nt]), flat_c, 0.0, ALU.mult, ALU.add))
            yield
            last = run[:, :, nt - 1]
            v(lambda e: e.tensor_copy(n_of[:, 0:1], last[:, 0:1]))
            v(lambda e: e.tensor_tensor(n_of[:, 1:E], last[:, 1:E], last[:, 0:E - 1], ALU.subtract))
            v(lambda e: e.tensor_scalar(tmp, n_of, float(P - 1), None, ALU.add))
            v(lambda e: e.tensor_copy(e8i[:, :], tmp))
            yield
            v(lambda e: e.tensor_scalar(e8i[:, :], e8i[:, :], P.bit_length() - 1, None, ALU.logical_shift_right))
            v(lambda e: e.tensor_copy(tiles_e, e8i[:, :]))
            v(lambda e: e.tensor_tensor_scan(ends, ones[:, 0:E], tiles_e, 0.0, ALU.mult, ALU.add))
            yield
            v(lambda e: e.tensor_tensor(tmp, ends, tiles_e, ALU.subtract))
            v(lambda e: e.scalar_tensor_tensor(out=start, in0=tmp, scalar=float(P), in1=last, op0=ALU.mult, op1=ALU.subtract))
            v(lambda e: e.tensor_tensor(start, start, n_of, ALU.add))
            yield
            v(lambda e: e.tensor_tensor(run, run, cnt, ALU.subtract))
            v(lambda e: e.tensor_tensor(run, run, start.unsqueeze(2).to_broadcast([P, E, nt]), ALU.add))
            yield
            v(lambda e: e.tensor_tensor(flat_r, flat_r, ranks[:, 0:E * nt], ALU.add))
            yield
            for k in range(K):
                v(lambda e, k=k: e.tensor_tensor(cnt, run, hot[k][:, :, t0:t0 + nt], ALU.mult))
                yield
                v(lambda e: e.tensor_reduce(picks[:, 0:nt], cnt.rearrange("p e i -> p i e"), AX.X, ALU.add))
                placed = v(lambda e, k=k: e.tensor_copy(slot_of[k][:, t0:t0 + nt], picks[:, 0:nt]))
                yield
            cmp = compared[:, 0:nj, :]
            v(lambda e: e.tensor_tensor(cmp, tile_no[:, 0:nj].unsqueeze(2).to_broadcast([1, nj, E]), ends[0:1, :].unsqueeze(1).to_broadcast([1, nj, E]), ALU.is_ge), [consts_in])
            yield
            v(lambda e: e.tensor_reduce(tile_expert[:, 0:nj], cmp, AX.X, ALU.add))
            v(lambda e: e.tensor_scalar(tile_expert[:, 0:nj], tile_expert[:, 0:nj], float(E - 1), None, ALU.min))
            tiles_known[n] = v(lambda e: e.tensor_copy(expert_of[n][:, :], tile_expert[:, 0:nj]))
            held["slots"] = (tiles_known[n],)
            yield
            for t in range(t0, t0 + nt):
                for k in range(K):
                    pool.wait(placed, zeroed, x1_in[b1 - 1])
                    s_scatter[n].count += 16
                    pool.steps.append(lambda e, t=t, k=k: e.indirect_dma_start(
                        sorted_x[n], bass.IndirectOffsetOnAxis(ap=slot_of[k][:, t:t + 1], axis=0), X1[:, t, :], None).then_inc(s_scatter[n].sem, 16))
                    yield
            scattered[n] = (s_scatter[n].sem, s_scatter[n].count)

        units = [(b, g) for b in range(B) for g in range(G4)]
        ahead = maxima()
        preparing = chained(prepare(b) for b in range(1, B))
        for _ in range(LEAD):
            Slot.now += 1
            next(ahead)
            next(preparing)
        collecting = []
        later = []
        W1 = Region(nc, experts_at).place("W1_sb", [P, E, FF])
        W2 = Region(nc, experts_at + 4 * E * FF).place("W2_sb", [P, E, NF, D])
        b2_rows = Region(nc, b2_at).place("b2_rows", [P, E, D])
        assert B % 2 == 0

        def step_first(parts):
            while parts:
                if next(parts[0], "ended") != "ended":
                    return
                parts.pop(0)

        def step_later():
            step_first(collecting)
            step_first(later)

        def after_collect(b):
            while collected[b] < G4:
                yield
            yield from pause(2)
            yield from finish(b)

        for n, (b, g) in enumerate(units):
            s = b % 2
            acc = pv_banks.take()

            def values(kt, slots):
                for G, (slot, mark) in enumerate(slots):
                    h = g * G4 + G
                    last = pe.do(lambda e, G=G, h=h, t=slot, s=s, acc=acc: e.matmul(
                        acc.ap[32 * G:32 * G + 32, :], vaug[s][:, kt, h, :], t.ap[:, :], start=kt == 0, stop=kt == TB - 1),
                        [mark, ready[b][1], *acc.free])
                    slot.free = (last,)
                return last

            waiting = None
            for kt in range(TB):
                slots = []
                for G in range(G4):
                    h = g * G4 + G
                    bank, slot = score_banks.take(), PT.take()
                    p_s = pe.do(lambda e, G=G, h=h, kt=kt, k=bank, s=s: e.matmul(k.ap, KS[s][:, G, kt * P:(kt + 1) * P], QS[s][:, h, :], start=True, stop=True),
                                [sent[n], *bank.free])
                    m = act.do(lambda e, k=bank, t=slot: e.activation(t.ap[:, :], k.ap, ACT.Exp, scale=SCORE_SCALE), [p_s, *slot.free])
                    bank.free = (m,)
                    slots.append((slot, m))
                    if waiting and G == PV_AT:
                        values(*waiting)
                    Slot.now += 1
                    next(preparing, None)
                    next(ahead, None)
                    step_later()
                waiting = (kt, slots)
            last = values(*waiting)
            t_in = act.do(lambda e, k=acc: e.activation(oT[:, :], k.ap, ACT.Copy), [last, *held["oT"]])
            acc.free = (t_in,)
            collecting.append(collect(b, g, t_in))
            if g == G4 - 1:
                v_read[s] = stack_read[s] = (last,)
                left.add(b)
                later += [after_collect(b), route(b)]
                if b == GROUPS[0][1] - 1:
                    later.append(sort_tokens(0, misc))
                if b == B - 2:
                    for e_ in range(E):
                        sp.dma(s_moe, W1[:, e_, :], a["W1"][e_], [last])
                        sp.dma(s_moe, W2[:, e_, :, :], a["W2"][e_].rearrange("(f p) d -> p f d", p=P))
                    moe_in = sp.dma(s_moe, b2_rows[:, :, :], a["b2"].partition_broadcast(P))

        units_done = [last, t_in]
        end = Region(nc, late_at)
        xs = Ring([Slot(end.place(f"xs{i}", [P, D])) for i in range(AHEAD)])
        xsT = Ring([Slot(end.place(f"xsT{i}", [P, P])) for i in range(2)])
        raw = Ring([Slot(end.place(f"raw{i}", [P, FF])) for i in range(2)])
        act_h = Ring([Slot(end.place(f"act_h{i}", [P, NF, P])) for i in range(2)])
        ys = Ring([Slot(end.place(f"ys{i}", [P, D])) for i in range(4)])
        back = [end.place(f"back{k}", [P, BACKS, TB, D]) for k in range(K)]
        fin = end.place("fin", [P, 2, TB, D])
        stats_c = end.place("stats_c", [P, 2, TB, 6])
        mv_c = end.place("mv_c", [P, 2, TB, 2])
        rstd_c = end.place("rstd_c", [P, 2, TB])
        assert end.at <= rest_at
        x_banks, h_banks, ht_banks = Ring(banks[0:1]), Ring(banks[1:3]), Ring(banks[3:5])
        y_banks = Ring([banks[5]])
        misc.rest = 0
        while collecting or later and scattered.get(0) is None:
            step_later()
        for bank in banks[0:6]:
            bank.free = (*bank.free, *units_done)
        for ring in (xs, xsT, raw, act_h, ys):
            for slot in ring.slots:
                slot.free = (*units_done,)
        later.append(sort_tokens(1, misc))
        stored, gathered, combined, shifted = [{}, {}], {}, set(), {}

        def expert_tiles():
            order = [(n, j) for n, t in enumerate(tiles_of) for j in range(t)]
            live, numbers = {}, {}

            def expert(engine, at):
                n, j = order[at]
                j0, nj = j // NUMBERS * NUMBERS, tiles_of[n]
                key = (engine, n, j0)
                if key not in numbers:
                    _, numbers[key] = nc.values_load_multi_w_load_instructions(
                        expert_of[n][0:1, j0:min(nj, j0 + NUMBERS)], engines=[engine], min_val=0, max_val=E - 1,
                        skip_runtime_bounds_check_because="sort_tokens counts at most E ends and caps the number at E - 1")
                return numbers[key][j - j0]

            def load(j):
                slot = xs.take()
                n, at = order[j]
                live[j] = {"x": slot, "x_in": sp.dma(s_load[j % AHEAD], slot.ap[:, :], sorted_x[n][at * P:(at + 1) * P, :], [scattered[n], *slot.free])}

            def turn(j):
                t, bank, slot = live[j], x_banks.take(), xsT.take()
                p = pe.do(lambda e: e.transpose(bank.ap[:, 0:P], t["x"].ap[:, :], ident[:, :]), [t["x_in"], *bank.free])
                t["x"].free = (p,)
                t["xT"], t["xT_in"] = slot, dve.do(lambda e: e.tensor_copy(slot.ap[:, :], bank.ap[:, 0:P]), [p, *slot.free])
                bank.free = (t["xT_in"],)

            def up(j):
                t, bank, slot = live[j], h_banks.take(), raw.take()
                pe.wait(t["xT_in"], moe_in, tiles_known[order[j][0]], *bank.free)

                def product(e):
                    return e.matmul(bank.ap, t["xT"].ap[:, :], W1[:, bass.ds(expert(mybir.EngineType.PE, j), 1), :].rearrange("p o f -> p (o f)"), start=True, stop=True)
                p = pe.do(product)
                t["xT"].free = (p,)
                t["raw"], t["raw_in"] = slot, dve.do(lambda e: e.tensor_copy(slot.ap[:, :], bank.ap), [p, *slot.free])
                bank.free = (t["raw_in"],)

            def turn_hidden(j):
                t, bank, slot = live[j], ht_banks.take(), act_h.take()
                p = transpose_tiles(lambda f: t["raw"].ap[:, f * P:(f + 1) * P], bank, [t["raw_in"]])
                t["raw"].free = (p,)
                act.wait(p, tiles_known[order[j][0]], *slot.free)
                for f in range(NF):
                    def gelu(e, f=f):
                        return e.activation(slot.ap[:, f, :], bank.ap[:, f * P:(f + 1) * P], ACT.Gelu,
                                            bias=b1c[:, bass.ds(expert(mybir.EngineType.Activation, j), 1), f:f + 1].rearrange("p o f -> p (o f)"))
                    m = act.do(gelu)
                bank.free = (m,)
                t["h"], t["h_in"] = slot, m

            def down(j):
                t, bank, slot = live.pop(j), y_banks.take(), ys.take()
                for f in range(NF):
                    p = pe.do(lambda e, f=f: e.matmul(bank.ap[:, 0:D], t["h"].ap[:, f, :], W2[:, bass.ds(expert(mybir.EngineType.PE, j), 1), f, :].rearrange("p o d -> p (o d)"),
                                                     start=f == 0, stop=f == NF - 1), [t["h_in"], *bank.free], signal=f == NF - 1)
                t["h"].free = (p,)

                def add_b2(e):
                    return e.tensor_tensor(slot.ap[:, :], bank.ap[:, 0:D], b2_rows[:, bass.ds(expert(mybir.EngineType.DVE, j), 1), :].rearrange("p o d -> p (o d)"), ALU.add)
                m = dve.do(add_b2, [p, moe_in, tiles_known[order[j][0]], *slot.free])
                bank.free = (m,)
                n, at = order[j]
                out_mark = sp.dma(s_store[n][j % 4], sorted_y[n][at * P:(at + 1) * P, :], slot.ap[:, :], [m])
                slot.free = (out_mark,)
                stored[n][j % 4] = out_mark

            for j in range(len(order) + AHEAD + 1):
                for lead, stage in ((0, load), (AHEAD - 2, turn), (AHEAD - 1, up), (AHEAD, turn_hidden), (AHEAD + 1, down)):
                    if 0 <= j - lead < len(order):
                        stage(j - lead)
                yield

        def shift_residual(b):
            shifted[b] = dve.do(lambda e: e.tensor_tensor(tiles(X, b), tiles(X, b), over_tiles(rows[:, b, GBE, :]), ALU.add), [made_ready["gg"]])
            yield
            yield

        def gather(b, n):
            s = b % BACKS
            while b >= BACKS and b - BACKS not in combined:
                yield
            for k in range(K):
                for i in range(TB):
                    pool.wait(*stored[n].values(), *back_free[s])
                    s_gather[s][k].count += 16
                    pool.steps.append(lambda e, k=k, i=i: e.indirect_dma_start(
                        back[k][:, s, i, :], None, sorted_y[n], bass.IndirectOffsetOnAxis(ap=slot_of[k][:, b * TB + i:b * TB + i + 1], axis=0)).then_inc(s_gather[s][k].sem, 16))
                    yield
            gathered[b] = [(t.sem, t.count) for t in s_gather[s]]

        def combine(b):
            s = b % 2
            t0 = b * TB
            while b not in gathered:
                yield
            yield from pause(GATHER_TIME if b < GROUPS[1][0] else 1)
            fetched = gathered[b]
            for k in range(K):
                for i in range(TB):
                    m = dve.do(lambda e, k=k, i=i: e.scalar_tensor_tensor(
                        out=X1[:, t0 + i, :], in0=back[k][:, b % BACKS, i, :], scalar=share[k][:, t0 + i:t0 + i + 1], in1=X1[:, t0 + i, :],
                        op0=ALU.mult, op1=ALU.add), [fetched[k], x1_in[b], (dve.sem, dve.count - TB + 1)] if k else [fetched[k], x1_in[b]])
                yield
            back_free[b % BACKS] = (m,)
            combined.add(b)
            normed = yield from normalise(tiles(X1, b), fin[:, s], stats_c[:, s], mv_c[:, s], rstd_c[:, s], [m], fin_free[s])
            m = dve.do(lambda e: e.tensor_tensor(fin[:, s], fin[:, s], over_tiles(rows[:, b, GG, :]), ALU.mult), [normed])
            yield
            m = dve.do(lambda e: e.tensor_tensor(fin[:, s], fin[:, s], tiles(X, b), ALU.add), [m, shifted[b]])
            yield from pause(4)
            fin_free[s] = (sp.dma(s_out[s], out_tiles[b], fin[:, s], [m]),)
            yield

        back_free, fin_free = [tuple(units_done)] * BACKS, [(), ()]
        later += [shift_residual(b) for b in range(B)]
        gathering = []

        def step_gathering():
            step_first(gathering)

        tiles_run = expert_tiles()
        for _ in range(AHEAD):
            next(tiles_run)
        for j, _ in enumerate(tiles_run, AHEAD):
            if j == tiles_of[0] + AHEAD + 1:
                gathering += [gather(b, 0) for b in range(*GROUPS[0])]
                later.append(beside([combine(b) for b in range(*GROUPS[0])], 2))
            for side in (step_later, step_gathering, step_later, step_gathering, step_later):
                side()
        gathering += [gather(b, 1) for b in range(*GROUPS[1])]
        later.append(beside([combine(b) for b in range(*GROUPS[1])], 2))
        while later or gathering:
            step_first(gathering)
            step_later()
        sp.wait(*[(t.sem, t.count) for t in s_out])

        block = scope.enter_context(nc.Block())

        @block.sync
        def _(engine):
            sp.play(engine)

        @block.scalar
        def _(engine):
            act.play(engine)

        @block.vector
        def _(engine):
            dve.play(engine)

        @block.gpsimd
        def _(engine):
            pool.play(engine)

        @block.tensor
        def _(engine):
            pe.play(engine)


def _layout(inputs):
    import numpy as np

    g = {k: np.asarray(v) for k, v in inputs.items()}
    B, L, D = g["L0_attn_x"].shape
    E, _, FF = g["L0_ffn_W1"].shape
    H, HD = 16, D // 16
    order = np.array([(4 * gg + G) * HD + d for gg in range(4) for d in range(HD) for G in range(4)])
    swap = np.array([(c // HD) * HD + (c % HD + HD // 2) % HD for c in range(D)])
    rot = swap[order]
    d_of = order % HD
    inv = 1.0 / 10000.0 ** (np.arange(0, HD, 2, dtype=np.float32) / np.float32(HD))
    freqs = (np.arange(L, dtype=np.float32)[:, None] * inv.astype(np.float32)[None, :]).astype(np.float32)
    emb = np.concatenate([freqs, freqs], -1)
    cos, sin = np.cos(emb).astype(np.float32), np.sin(emb).astype(np.float32)
    sign = np.where(d_of < HD // 2, -1.0, 1.0).astype(np.float32)
    c = np.ascontiguousarray
    Wi = g["L0_attn_W_in"]
    f32 = lambda *parts: c(np.concatenate(parts, 1))
    flat = lambda w: w.reshape(w.shape[0], -1)
    return {
        "x": c(g["L0_attn_x"]), "first_pack": f32(g["L0_c"].T, g["L0_wmod"]), "ident": np.eye(D, dtype=np.float32),
        "ssm_pack": f32(Wi[:D], Wi[D:].T, g["L0_attn_W_state"].T, g["L0_attn_W_dt"].T, g["L0_attn_W_C"].T, g["L0_attn_W_out"].T),
        "vecs": c(np.stack([g["L0_attn_b_dt"], g["L0_attn_A_log"], g["L0_attn_D"], g["L0_ffn_bq"][order], g["L0_ffn_bq"][rot],
                            g["L0_ffn_bk"][order], g["L0_ffn_bk"][rot], g["L0_ffn_bv"]], 1)),
        "row_pack": np.concatenate([g["L0_ffn_bo"], g["L0_ffn_g1"], g["L0_ffn_be1"], g["L0_ffn_g2"], g["L0_ffn_be2"],
                                    g["L0_ffn_bg"], np.arange(E, 0, -1).astype(np.float32)]),
        "consts": f32(g["L0_ffn_Wq"][:, order], g["L0_ffn_Wq"][:, rot], g["L0_ffn_Wk"][:, order], g["L0_ffn_Wk"][:, rot],
                      g["L0_ffn_Wv"], g["L0_ffn_Wo"], cos.T[d_of], sin.T[d_of] * sign[:, None],
                      np.triu(np.ones((D, D), np.float32), 1), g["L0_ffn_Wg"],
                      flat(g["L0_ffn_b1"].reshape(E, FF // D, D).transpose(2, 0, 1))),
        "tile_no": np.arange(2 * B * L // D + E, dtype=np.float32)[None],
        "W1": c(g["L0_ffn_W1"]), "W2": c(g["L0_ffn_W2"]), "b2": c(g["L0_ffn_b2"]),
    }


def kernel(**inputs):
    import concourse.bacc as _bacc
    from concourse import mybir as _mybir
    from concourse.bass_utils import run_bass_kernel_spmd as _run

    arrays = _layout(inputs)
    nc = _bacc.Bacc("TRN2", target_bir_lowering=False, num_devices=1)
    aps = {k: nc.dram_tensor(f"in_{k}", v.shape, _mybir.dt.from_np(v.dtype), kind="ExternalInput").ap() for k, v in arrays.items()}
    out = nc.dram_tensor("out_0", arrays["x"].shape, _mybir.dt.float32, kind="ExternalOutput").ap()
    adaln_block(nc, aps, out)
    r = _run(nc, [{f"in_{k}": v for k, v in arrays.items()}], core_ids=[0])
    return r.results[0]["out_0"]
```
